# Optimizing a Trainium2 kernel written in Bass

```python
import numpy as np
import jax
import jax.numpy as jnp

def _softmax(x, axis=-1):
    return jax.nn.softmax(x, axis=axis)

def _gelu(x):
    return jax.nn.gelu(x, approximate=True)

def _silu(x):
    return jax.nn.silu(x)

def _sigmoid(x):
    return jax.nn.sigmoid(x)

def _layernorm(x, axis=-1, eps=1e-05):
    m = jnp.mean(x, axis=axis, keepdims=True)
    v = jnp.var(x, axis=axis, keepdims=True)
    return (x - m) / jnp.sqrt(v + eps)

def _scatter_add(tgt, idx, src, axis=0):
    return tgt.at[idx].add(src)

def _segment_sum(src, seg, n):
    return jax.ops.segment_sum(src, seg, n)
kernel_name = 'mk_adj_resnorm_d2_adj_r2_c195c5'

def setup_inputs(seed: int=0):
    np.random.seed(seed)
    _w = jnp.asarray

    def _rec_inputs():
        import jax
        import jax.numpy as jnp
        _gk = jax.random.key(seed)
        x = -0.0002928 + 1 * jax.random.normal(jax.random.fold_in(_gk, 1), (16, 512, 256), jnp.float32)
        _a = jax.random.bernoulli(jax.random.fold_in(_gk, 2), 0.03125, (16, 512, 512))
        adj = _a.astype(jnp.int32)
        return (x, adj)
    x, adj = _rec_inputs()

    def _L0_gnn_setup():
        import jax, jax.numpy as jnp
        import numpy as np
        ALPHA = 0.2

        def _leaky(x):
            return jnp.where(x >= 0, x, ALPHA * x)
        key = jax.random.key(seed)
        k1, k2, k3, k4 = jax.random.split(key, 4)
        B, N, F_in, F_out = (4, 1024, 256, 256)
        h = jax.random.normal(k1, (B, N, F_in), dtype=jnp.float32)
        W = jax.random.normal(k2, (F_in, F_out), dtype=jnp.float32) * 0.05
        a = jax.random.normal(k3, (2 * F_out, 1), dtype=jnp.float32) * 0.05
        adj = jax.random.randint(k4, (B, N, N), 0, 2, dtype=jnp.int32)
        return {'h': h, 'W': W, 'a': a, 'adj': adj}
    _L0_gnn_all = _L0_gnn_setup()
    _L0_gnn_in = {k: v for k, v in _L0_gnn_all.items() if k in ('W', 'a')}
    del _L0_gnn_all

    def _L1_gnn_setup():
        import jax, jax.numpy as jnp
        import numpy as np
        NEG_INF = -1000000000.0
        NEG_SLOPE = 0.2

        def gat_layer(x, mask, W, a_src, a_dst, bias, concat):
            B, N, _ = x.shape
            H, F = a_src.shape
            xl = (x @ W).reshape(B, N, H, F)
            asrc = jnp.einsum('bnhf,hf->bnh', xl, a_src)
            adst = jnp.einsum('bnhf,hf->bnh', xl, a_dst)
            e = jax.nn.leaky_relu(asrc[:, :, None, :] + adst[:, None, :, :], NEG_SLOPE)
            e = jnp.where(mask[..., None], e, NEG_INF)
            attn = jax.nn.softmax(e, axis=1)
            out = jnp.einsum('bsdh,bshf->bdhf', attn, xl)
            if concat:
                out = out.reshape(B, N, H * F)
            else:
                out = out.mean(axis=2)
            return out + bias
        key = jax.random.key(seed)
        ks = jax.random.split(key, 10)
        B, N, Din, Fh, H, Dout = (8, 512, 256, 128, 4, 256)
        s = 0.05
        return {'adj': jax.random.randint(ks[0], (B, N, N), 0, 2, dtype=jnp.int32), 'x': jax.random.normal(ks[1], (B, N, Din), dtype=jnp.float32), 'W1': jax.random.normal(ks[2], (Din, H * Fh), dtype=jnp.float32) * s, 'att_src1': jax.random.normal(ks[3], (H, Fh), dtype=jnp.float32) * s, 'att_dst1': jax.random.normal(ks[4], (H, Fh), dtype=jnp.float32) * s, 'b1': jax.random.normal(ks[5], (H * Fh,), dtype=jnp.float32) * s, 'W2': jax.random.normal(ks[6], (H * Fh, Dout), dtype=jnp.float32) * s, 'att_src2': jax.random.normal(ks[7], (1, Dout), dtype=jnp.float32) * s, 'att_dst2': jax.random.normal(ks[8], (1, Dout), dtype=jnp.float32) * s, 'b2': jax.random.normal(ks[9], (Dout,), dtype=jnp.float32) * s}
    _L1_gnn_all = _L1_gnn_setup()
    _L1_gnn_in = {k: v for k, v in _L1_gnn_all.items() if k in ('W1', 'att_src1', 'att_dst1', 'b1', 'W2', 'att_src2', 'att_dst2', 'b2')}
    del _L1_gnn_all
    return {'x': x, 'adj': adj, 'L0_gnn_W': _L0_gnn_in['W'], 'L0_gnn_a': _L0_gnn_in['a'], 'L1_gnn_W1': _L1_gnn_in['W1'], 'L1_gnn_att_src1': _L1_gnn_in['att_src1'], 'L1_gnn_att_dst1': _L1_gnn_in['att_dst1'], 'L1_gnn_b1': _L1_gnn_in['b1'], 'L1_gnn_W2': _L1_gnn_in['W2'], 'L1_gnn_att_src2': _L1_gnn_in['att_src2'], 'L1_gnn_att_dst2': _L1_gnn_in['att_dst2'], 'L1_gnn_b2': _L1_gnn_in['b2']}

def reference(x, adj, L0_gnn_W, L0_gnn_a, L1_gnn_W1, L1_gnn_att_src1, L1_gnn_att_dst1, L1_gnn_b1, L1_gnn_W2, L1_gnn_att_src2, L1_gnn_att_dst2, L1_gnn_b2):
    import jax
    import jax.numpy as jnp

    def _L0_gnn_ref(h, W, a, adj):
        import jax, jax.numpy as jnp
        import numpy as np
        ALPHA = 0.2

        def _leaky(x):
            return jnp.where(x >= 0, x, ALPHA * x)
        F_out = W.shape[1]
        Wh = jnp.matmul(h, W)
        Wh_sg = jax.lax.stop_gradient(Wh)
        a1 = a[:F_out, 0]
        a2 = a[F_out:, 0]
        s_i = Wh_sg @ a1
        s_j = Wh_sg @ a2
        e = _leaky(s_i[:, :, None] + s_j[:, None, :])
        e = jnp.where(adj > 0, e, jnp.float32(-9000000000000000.0))
        attention = jax.nn.softmax(e, axis=1)
        h_prime = jnp.einsum('bij,bjf->bif', attention, Wh)
        return _leaky(h_prime)

    def _L1_gnn_ref(adj, x, W1, att_src1, att_dst1, b1, W2, att_src2, att_dst2, b2):
        import jax, jax.numpy as jnp
        import numpy as np
        NEG_INF = -1000000000.0
        NEG_SLOPE = 0.2

        def gat_layer(x, mask, W, a_src, a_dst, bias, concat):
            B, N, _ = x.shape
            H, F = a_src.shape
            xl = (x @ W).reshape(B, N, H, F)
            asrc = jnp.einsum('bnhf,hf->bnh', xl, a_src)
            adst = jnp.einsum('bnhf,hf->bnh', xl, a_dst)
            e = jax.nn.leaky_relu(asrc[:, :, None, :] + adst[:, None, :, :], NEG_SLOPE)
            e = jnp.where(mask[..., None], e, NEG_INF)
            attn = jax.nn.softmax(e, axis=1)
            out = jnp.einsum('bsdh,bshf->bdhf', attn, xl)
            if concat:
                out = out.reshape(B, N, H * F)
            else:
                out = out.mean(axis=2)
            return out + bias
        B, N, _ = adj.shape
        mask = (adj > 0) | jnp.eye(N, dtype=bool)[None]
        h = jax.nn.elu(gat_layer(x, mask, W1, att_src1, att_dst1, b1, concat=True))
        h = gat_layer(h, mask, W2, att_src2, att_dst2, b2, concat=False)
        return h
    x = _layernorm(x + _L0_gnn_ref(x, L0_gnn_W, L0_gnn_a, adj), axis=-1)
    x = _layernorm(x + _L1_gnn_ref(adj, x, L1_gnn_W1, L1_gnn_att_src1, L1_gnn_att_dst1, L1_gnn_b1, L1_gnn_W2, L1_gnn_att_src2, L1_gnn_att_dst2, L1_gnn_b2), axis=-1)
    return x

_drawn_inputs = setup_inputs


def setup_inputs(seed=0):
    import zlib

    import numpy as np

    out = dict(_drawn_inputs(seed))
    spreads = {}
    factors = {'L1_gnn_att_dst1': 8.0, 'L1_gnn_att_src2': 7.923, 'L1_gnn_att_dst2': 8.0}
    for name, (base, spread) in spreads.items():
        noise = np.random.default_rng([zlib.crc32(name.encode()), seed]).standard_normal(out[name].shape)
        drawn = base * np.exp(spread * noise) if base else spread * noise
        out[name] = jnp.asarray(drawn.astype(out[name].dtype))
    for name, factor in factors.items():
        out[name] = (out[name] * factor).astype(out[name].dtype)
    return out
```

```python
from contextlib import ExitStack

import concourse.bass as bass
from concourse import mybir

F32 = mybir.dt.float32
BF16 = mybir.dt.bfloat16
I32 = mybir.dt.int32
ALU = mybir.AluOpType
ACT = mybir.ActivationFunctionType

P = 128
SLOPE = 0.2
EPS = 1e-5
NO_EDGE = -9.0e15
LOWEST = -3.0e38

A_X, A_MASK, A_LOGIT, A_VALUES, A_OUT, A_TURNS = range(6)
B_X1T, B_XL, B_HEADS, B_HT, C_XL, C_OUT, O_TURNS = 0, 1, 3, 7, 9, 10, 12
COLS1, AROW1, VROW1, COLS2, AROW2, VROW2, SMALL_TURNS = range(7)
ROW_TURNS, V2_TURNS = 5, 5
A_STEPS, B_STEPS = 13, 37


def nth(per_graph, g, k):
    return g * per_graph + (k + 1)


class Steps:

    def __init__(self, engine, semaphore, per_graph):
        self.engine, self.semaphore, self.per_graph = engine, semaphore, per_graph

    def begin(self, g):
        self.g, self.k = g, 0

    def done(self, instruction):
        instruction.then_inc(self.semaphore, 1)
        self.k += 1

    def wait(self):
        self.engine.wait_ge(self.semaphore, nth(self.per_graph, self.g, self.k - 1))

    def end(self):
        assert self.k == self.per_graph, (self.semaphore, self.k)


def build(nc, x, adj, w0, a0, w1, src1, dst1, b1, w2, src2, dst2, b2, out):
    G, N, F = x.shape
    NB = N // P
    KF = F // P
    H = src1.shape[0]
    D = src1.shape[1]
    HD = H * D
    KH = HD // P
    assert N == 512 and D == P and F == 256 and H == 4 and G % 2 == 0

    with ExitStack() as ctx:
        def sb(name, shape, dt=F32):
            return ctx.enter_context(nc.sbuf_tensor(name, shape, dt))

        def bank(name):
            return ctx.enter_context(nc.psum_tensor(name, [P, 512], F32))

        def sem(name):
            return ctx.enter_context(nc.semaphore(name))

        ident = sb("ident", [P, P])
        ident_b = sb("ident_b", [P, P], BF16)
        off_diag = sb("off_diag", [P, P], BF16)
        ones = sb("ones", [P, P])
        pick_a1 = sb("pick_a1", [3 * H, H, P], BF16)
        pick_v1 = sb("pick_v1", [6 * H, 2 * H, P], BF16)
        pick_a2 = sb("pick_a2", [3, 1, P], BF16)
        pick_v2 = sb("pick_v2", [6, 2, P], BF16)
        w0_t = sb("w0_t", [P, KF, F])
        w1_t = sb("w1_t", [P, KF, HD])
        w2_t = sb("w2_t", [P, KH, F])
        vec0 = sb("vec0", [P, 2, F])
        vec1 = sb("vec1", [P, 2, HD])
        vec2 = sb("vec2", [P, 2, F])
        wa0 = sb("wa0", [P, KF, 2])
        wa1 = sb("wa1", [P, KF, 2 * H])
        wa2 = sb("wa2", [P, KH, 2])
        wa0_wide = sb("wa0_wide", [P, KF, P])
        bias_row = sb("bias_row", [1, HD + F])
        bias_rest = sb("bias_rest", [1, HD + F])
        bias_parts = sb("bias_parts", [1, 3, HD + F], BF16)
        bias3 = sb("bias3", [3, HD + F], BF16)
        ones3 = sb("ones3", [3, P], BF16)
        minus_half = sb("minus_half", [P, NB])
        scratch = sb("scratch", [P, N])
        gate_t = sb("gate_t", [P, 8])

        x_t = [sb(f"x{i}", [P, NB, F]) for i in range(2)]
        adj_t = [sb(f"adj{i}", [P, NB, N], I32) for i in range(2)]
        mask = [sb(f"mask{i}", [P, NB, N], BF16) for i in range(2)]
        mask_T = [sb(f"mask_T{i}", [P, NB, N], BF16) for i in range(2)]
        x1 = [sb(f"x1_{i}", [P, NB, F]) for i in range(2)]
        xT = sb("xT", [P, KF, N])
        sj = sb("sj", [P, 2, NB])
        edge0 = sb("edge0", [P, NB, N])
        weight0 = sb("weight0", [P, NB, N])
        top0 = sb("top0", [P, NB])
        neg_top0 = sb("neg_top0", [P, NB])
        den0 = sb("den0", [P, NB])
        rden0 = sb("rden0", [P, NB])
        values0 = sb("values0", [P, NB, F])
        mix0 = sb("mix0", [P, NB, F])
        leak0 = sb("leak0", [P, NB, F])
        stats = sb("stats", [P, NB, 6])
        moments = sb("moments", [P, NB, 2])
        var_eps = sb("var_eps", [P, NB])
        rstd = sb("rstd", [P, NB])
        x1T = sb("x1T", [P, KF, N])
        ab = sb("ab", [P, NB, 2 * H])
        ab2 = sb("ab2", [P, NB, 2])
        a_low = sb("a_low", [P, NB, H])
        a2_low = sb("a2_low", [P, NB, 1])
        rest = sb("rest", [P, NB, 2 * H])
        a_parts = sb("a_parts", [P, NB, 3 * H], BF16)
        v_parts = sb("v_parts", [P, NB, 6 * H], BF16)
        a2_parts = sb("a2_parts", [P, NB, 3], BF16)
        v2_parts = sb("v2_parts", [P, NB, 6], BF16)
        a_rows = sb("a_rows", [3 * H, N], BF16)
        v_rows = sb("v_rows", [6 * H, N], BF16)
        a2_rows = sb("a2_rows", [3, N], BF16)
        v2_rows = sb("v2_rows", [6, N], BF16)
        top = sb("top", [P, NB, H])
        shift = sb("shift", [P, NB, H])
        v = sb("v", [P, NB, 2 * H])
        junk = sb("junk", [P, 2, NB, N], BF16)
        xl1 = sb("xl1", [P, NB, H, D + 1])
        xl2 = sb("xl2", [P, NB, F + 1])
        logit = [sb(f"logit{i}", [P, NB, N]) for i in range(2)]
        prob = [sb(f"prob{i}", [P, NB, N]) for i in range(2)]
        rden = sb("rden", [P, NB])
        hid = sb("hid", [P, NB, HD])
        hid_T = sb("hid_T", [P, KH, N])
        y2 = sb("y2", [P, NB, F])
        stats2 = sb("stats2", [P, NB, 6])
        moments2 = sb("moments2", [P, NB, 2])
        var_eps2 = sb("var_eps2", [P, NB])
        rstd2 = sb("rstd2", [P, NB])
        out_t = sb("out_t", [P, NB, F])

        bank_a = [bank(f"bank_a{i}") for i in range(2)]
        bank_small = bank("bank_small")
        bank_row = [bank(f"bank_row{i}") for i in range(2)]
        bank_v2 = bank("bank_v2")
        bank_o = [bank(f"bank_o{i}") for i in range(2)]

        a_full = [sem(f"a_full{i}") for i in range(2)]
        a_taken = [sem(f"a_taken{i}") for i in range(2)]
        small_full, small_taken = sem("small_full"), sem("small_taken")
        row_full = [sem(f"row_full{i}") for i in range(2)]
        row_taken = [sem(f"row_taken{i}") for i in range(2)]
        v2_full, v2_taken = sem("v2_full"), sem("v2_taken")
        o_full = [sem(f"o_full{i}") for i in range(2)]
        o_taken = [sem(f"o_taken{i}") for i in range(2)]

        weights_in = sem("weights_in")
        bias_parts_ready = sem("bias_parts_ready")
        bias3_in = sem("bias3_in")
        pool_consts = sem("pool_consts")
        vector_consts = sem("vector_consts")
        x_in = [sem(f"x_in{i}") for i in range(2)]
        adj_in = [sem(f"adj_in{i}") for i in range(2)]
        out_stored = [sem(f"out_stored{i}") for i in range(2)]
        mask_ready = sem("mask_ready")
        self_edges = sem("self_edges")
        low0_ready = sem("low0_ready")
        masked0_ready = sem("masked0_ready")
        prob0_ready = sem("prob0_ready")
        rden0_ready = sem("rden0_ready")
        leak0_ready = sem("leak0_ready")
        sum0_ready = sem("sum0_ready")
        var_ready = sem("var_ready")
        rstd_ready = sem("rstd_ready")
        x1_ready = sem("x1_ready")
        a_steps = sem("a_steps")
        b_steps = sem("b_steps")
        parts_ready = sem("parts_ready")
        a_low_ready = sem("a_low_ready")
        low_ready = sem("low_ready")
        masked_ready = sem("masked_ready")
        prob_ready = sem("prob_ready")
        rden_ready = sem("rden_ready")
        exp_h_ready = sem("exp_h_ready")
        hid_ready = sem("hid_ready")
        var2_ready = sem("var2_ready")
        rstd2_ready = sem("rstd2_ready")
        out_ready = sem("out_ready")

        POOL_CONSTS, VECTOR_CONSTS = 26, 4 + 2 * (KF * (1 + H) + KH) + KF
        WEIGHTS = 8 * 16

        block = ctx.enter_context(nc.Block())

        def schedule(engine, stage_a, stage_bc):
            for piece in range(4):
                stage_a(0, 0, piece)
            stage_bc(0, 0, stage_a)
            with engine.Fori(1, G - 1, 2) as i:
                stage_bc(i, 1, stage_a)
                stage_bc(i + 1, 0, stage_a)
            stage_bc(G - 1, 1, None)

        @block.sync
        def _(sp):
            for tile, src in (
                (w0_t[:], w0.rearrange("(k p) n -> p k n", p=P)),
                (w1_t[:], w1.rearrange("(k p) n -> p k n", p=P)),
                (w2_t[:], w2.rearrange("(k p) n -> p k n", p=P)),
                (vec0[:], a0.rearrange("(a t f) o -> a t (f o)", a=1, t=2).broadcast_to([P, 2, F])),
                (vec1[:, 0, :], src1.rearrange("(a h) f -> a (h f)", a=1).broadcast_to([P, HD])),
                (vec1[:, 1, :], dst1.rearrange("(a h) f -> a (h f)", a=1).broadcast_to([P, HD])),
                (vec2[:, 0, :], src2.broadcast_to([P, F])),
                (vec2[:, 1, :], dst2.broadcast_to([P, F])),
            ):
                sp.dma_start(tile, src).then_inc(weights_in, 16)
            sp.dma_start(bias_row[:, 0:HD], b1.rearrange("(a f) -> a f", a=1)).then_inc(bias3_in, 16)
            sp.dma_start(bias_row[:, HD:], b2.rearrange("(a f) -> a f", a=1)).then_inc(bias3_in, 16)

            def load(g, p, reused):
                if reused:
                    sp.wait_ge(mask_ready, nth(1, g - 2, 0))
                sp.dma_start(adj_t[p][:], adj[g].rearrange("(b p) n -> p b n", p=P)).then_inc(adj_in[p], 16)
                if reused:
                    sp.wait_ge(sum0_ready, nth(1, g - 2, 0))
                sp.dma_start(x_t[p][:], x[g].rearrange("(b p) n -> p b n", p=P)).then_inc(x_in[p], 16)

            def store(g, p):
                sp.wait_ge(out_ready, nth(1, g, 0))
                sp.dma_start(out[g].rearrange("(b p) n -> p b n", p=P), out_t[:]).then_inc(out_stored[p], 16)

            load(0, 0, False)
            load(1, 1, False)
            sp.wait_ge(bias_parts_ready, 1)
            sp.dma_start(bias3[:], bias_parts[:]).then_inc(bias3_in, 16)
            load(2, 0, True)
            store(0, 0)
            with sp.Fori(1, G - 3, 2) as i:
                load(i + 2, 1, True)
                store(i, 1)
                load(i + 3, 0, True)
                store(i + 1, 0)
            load(G - 1, 1, True)
            store(G - 3, 1)
            store(G - 2, 0)
            store(G - 1, 1)
            for p in range(2):
                sp.wait_ge(out_stored[p], 16 * (G // 2))

        @block.gpsimd
        def _(pool):
            count = [0]

            def const(instruction):
                instruction.then_inc(pool_consts, 1)
                count[0] += 1
                pool.wait_ge(pool_consts, count[0])

            const(nc.gpsimd.memset(ones[:], 1.0))
            const(nc.gpsimd.memset(ones3[:], 1.0))
            const(nc.gpsimd.memset(minus_half[:], -0.5))
            const(nc.gpsimd.memset(xl1[:, :, :, D:D + 1], 1.0))
            const(nc.gpsimd.memset(xl2[:, :, F:F + 1], 1.0))
            const(nc.gpsimd.memset(ident[:], 0.0))
            const(nc.gpsimd.affine_select(out=ident[:], in_=ident[:], compare_op=ALU.not_equal, fill=1.0,
                                          base=0, pattern=[[-1, P]], channel_multiplier=1))
            const(nc.gpsimd.tensor_copy(ident_b[:], ident[:]))
            const(nc.gpsimd.memset(off_diag[:], 1.0))
            const(nc.gpsimd.affine_select(out=off_diag[:], in_=off_diag[:], compare_op=ALU.not_equal,
                                          fill=0.0, base=0, pattern=[[-1, P]], channel_multiplier=1))
            for pick, q in ((pick_a1, H), (pick_v1, 2 * H), (pick_a2, 1), (pick_v2, 2)):
                const(nc.gpsimd.memset(pick[:], 0.0))
                for part in range(3):
                    const(nc.gpsimd.affine_select(out=pick[:], in_=pick[:], compare_op=ALU.not_equal,
                                                  fill=1.0, base=-part * q, pattern=[[-1, q], [0, P]],
                                                  channel_multiplier=1))
            assert count[0] == POOL_CONSTS
            pool.wait_ge(vector_consts, VECTOR_CONSTS)

            def norm(g, var_sem, var, rstd_t, rstd_sem):
                pool.wait_ge(var_sem, nth(1, g, 0))
                nc.gpsimd.tensor_tensor(rstd_t[:], var[:], minus_half[:], ALU.pow).then_inc(rstd_sem, 1)

            def stage_a(g, p, piece):
                if piece == 2:
                    pool.wait_ge(masked0_ready, nth(1, g, 0))
                    for m in (mask_T[p], mask[p]):
                        for b in range(NB):
                            d = m[:, b, b * P:(b + 1) * P]
                            last = nc.gpsimd.tensor_tensor(d, d, off_diag[:], ALU.mult)
                    last.then_inc(self_edges, 1)
                if piece == 3:
                    pool.wait_ge(leak0_ready, nth(1, g, 0))
                    nc.gpsimd.tensor_tensor(leak0[:], leak0[:], x_t[p][:], ALU.add).then_inc(sum0_ready, 1)
                    norm(g, var_ready, var_eps, rstd, rstd_ready)

            def masked(g, p, n):
                t = logit[n % 2]
                if n < 4:
                    pool.wait_ge(row_taken[n % 2], nth(ROW_TURNS, g, 2 + n // 2))
                else:
                    pool.wait_ge(row_taken[1], nth(ROW_TURNS, g, 4))
                for half in range(2):
                    s = slice(half * NB // 2, (half + 1) * NB // 2)
                    nc.gpsimd.tensor_tensor(t[:, s, :], t[:, s, :], mask[p][:, s, :],
                                            ALU.add).then_inc(masked_ready, 1)

            def stage_bc(g, p, stage_a):
                masked(g, p, 0)
                masked(g, p, 1)
                masked(g, p, 2)
                masked(g, p, 3)
                if stage_a:
                    stage_a(g + 1, 1 - p, 2)
                masked(g, p, 4)
                norm(g, var2_ready, var_eps2, rstd2, rstd2_ready)
                if stage_a:
                    stage_a(g + 1, 1 - p, 3)

            schedule(pool, stage_a, stage_bc)

        @block.scalar
        def _(act):
            act.wait_ge(vector_consts, VECTOR_CONSTS)
            act.wait_ge(pool_consts, POOL_CONSTS)

            def stage_a(g, p, piece):
                if piece == 0:
                    act.wait_ge(a_full[0], nth(A_TURNS, g, A_X))
                    nc.scalar.copy(xT[:, 0, :], bank_a[0][:]).then_inc(a_taken[0], 1)
                    act.wait_ge(a_full[0], nth(A_TURNS, g, A_MASK))
                    nc.scalar.copy(mask_T[p][:, 0:2, :], bank_a[0][:].bitcast(BF16)
                                   .rearrange("p (b n) -> p b n", b=2)).then_inc(a_taken[0], 1)
                if piece == 1:
                    act.wait_ge(a_full[1], nth(A_TURNS, g, A_LOGIT))
                    act.wait_ge(a_taken[0], nth(A_TURNS, g, A_LOGIT))
                    for b in range(NB):
                        last = nc.scalar.activation(edge0[:, b, :], bank_a[1][:], ACT.Identity,
                                                    bias=sj[:, 1, b:b + 1], scale=SLOPE)
                    last.then_inc(low0_ready, 1)
                if piece == 2:
                    act.wait_ge(masked0_ready, nth(1, g, 0))
                    for b in range(NB):
                        last = nc.scalar.activation(weight0[:, b, :], edge0[:, b, :], ACT.Exp,
                                                    bias=neg_top0[:, b:b + 1], accum_out=den0[:, b:b + 1])
                    last.then_inc(prob0_ready, 1)
                    act.wait_ge(rden0_ready, nth(1, g, 0))
                    for b in range(NB):
                        if b % 2 == 0:
                            act.wait_ge(a_full[b // 2], nth(A_TURNS, g, A_VALUES))
                        last = nc.scalar.activation(values0[:, b, :], bank_a[b // 2][:, (b % 2) * F:(b % 2 + 1) * F],
                                                    ACT.Copy, scale=rden0[:, b:b + 1])
                        if b % 2:
                            last.then_inc(a_taken[b // 2], 1)
                if piece == 3:
                    for i in range(2):
                        act.wait_ge(a_full[i], nth(A_TURNS, g, A_OUT))
                        nc.scalar.copy(mix0[:, 2 * i:2 * i + 2, :], bank_a[i][:]
                                       .rearrange("p (b f) -> p b f", b=2)).then_inc(a_taken[i], 1)

            def low(g, n, bias):
                act.wait_ge(v2_full, nth(V2_TURNS, g, n))
                act.wait_ge(a_low_ready, nth(2, g, n // H))
                for b in range(NB):
                    last = nc.scalar.activation(logit[n % 2][:, b, :], bank_v2[:], ACT.Identity, bias=bias(b))
                last.then_inc(low_ready, 1)

            def expo(g, n):
                for half in range(2):
                    s = slice(half * NB // 2, (half + 1) * NB // 2)
                    act.wait_ge(masked_ready, nth(10, g, 2 * n + half))
                    last = nc.scalar.activation(prob[n % 2][:, s, :], logit[n % 2][:, s, :], ACT.Exp)
                last.then_inc(prob_ready, 1)

            def free_prob(g, n):
                if n >= 2:
                    act.wait_ge(o_full[1], nth(O_TURNS, g, B_HEADS + n - 2))
                elif not (isinstance(g, int) and g == 0):
                    act.wait_ge(o_full[1], nth(O_TURNS, g - 1, C_OUT + 1 if n == 0 else B_HEADS + 3))

            def take_head(g, n):
                for i in range(2):
                    act.wait_ge(rden_ready, nth(8, g, 2 * n + i))
                    for j in range(2):
                        b = 2 * i + j
                        last = nc.scalar.activation(hid[:, b, n * D:(n + 1) * D],
                                                    bank_o[i][:, j * (D + 1):j * (D + 1) + D],
                                                    ACT.Copy, scale=rden[:, b:b + 1])
                    last.then_inc(o_taken[i], 1)

            def stage_bc(g, p, stage_a):
                act.wait_ge(o_full[0], nth(O_TURNS, g, B_X1T))
                nc.scalar.copy(x1T[:, 0, :], bank_o[0][:]).then_inc(o_taken[0], 1)
                for b in range(NB):
                    act.wait_ge(o_full[b % 2], nth(O_TURNS, g, B_XL + b // 2))
                    nc.scalar.copy(xl1[:, b, :, 0:D], bank_o[b % 2][:]
                                   .rearrange("p (h f) -> p h f", h=H)).then_inc(o_taken[b % 2], 1)
                if stage_a:
                    stage_a(g + 1, 1 - p, 0)
                def low1(n):
                    low(g, n, lambda b: a_low[:, b, n:n + 1])
                low1(0)
                low1(1)
                free_prob(g, 0)
                expo(g, 0)
                free_prob(g, 1)
                expo(g, 1)
                low1(2)
                take_head(g, 0)
                free_prob(g, 2)
                expo(g, 2)
                low1(3)
                take_head(g, 1)
                free_prob(g, 3)
                expo(g, 3)
                if stage_a:
                    stage_a(g + 1, 1 - p, 1)
                take_head(g, 2)
                take_head(g, 3)
                act.wait_ge(o_taken[1], nth(O_TURNS, g, B_HEADS + 3))
                nc.scalar.activation(logit[1][:], hid[:], ACT.Exp).then_inc(exp_h_ready, 1)
                for k in range(0, KH, 2):
                    act.wait_ge(o_full[0], nth(O_TURNS, g, B_HT + k // 2))
                    nc.scalar.copy(hid_T[:, k, :], bank_o[0][:]).then_inc(o_taken[0], 1)
                if stage_a:
                    stage_a(g + 1, 1 - p, 2)
                for i in range(2):
                    act.wait_ge(o_full[i], nth(O_TURNS, g, C_XL))
                    nc.scalar.copy(xl2[:, 2 * i:2 * i + 2, 0:F], bank_o[i][:]
                                   .rearrange("p (b f) -> p b f", b=2)).then_inc(o_taken[i], 1)
                low(g, 4, lambda b: a2_low[:, b, :])
                free_prob(g, 4)
                expo(g, 4)
                if stage_a:
                    stage_a(g + 1, 1 - p, 3)

            schedule(act, stage_a, stage_bc)

        @block.vector
        def _(dve):
            count = [0]

            def const(instruction):
                instruction.then_inc(vector_consts, 1)
                count[0] += 1
                dve.wait_ge(vector_consts, count[0])

            dve.wait_ge(bias3_in, 32)
            const(nc.vector.tensor_copy(bias_parts[:, 0, :], bias_row[:]))
            const(nc.vector.tensor_tensor(bias_rest[:], bias_row[:], bias_parts[:, 0, :], ALU.subtract))
            const(nc.vector.tensor_copy(bias_parts[:, 1, :], bias_rest[:]))
            const(nc.vector.tensor_tensor(bias_rest[:], bias_rest[:], bias_parts[:, 1, :], ALU.subtract))
            nc.vector.tensor_copy(bias_parts[:, 2, :], bias_rest[:]).then_inc(bias_parts_ready, 1)
            dve.wait_ge(weights_in, WEIGHTS)
            dve.wait_ge(pool_consts, POOL_CONSTS)

            def through(w, vec, dst):
                const(nc.vector.tensor_tensor_reduce(scratch[:, 0:w.shape[-1]], w, vec, 1.0, 0.0, ALU.mult,
                                                     ALU.add, dst))
            for t in range(2):
                for k in range(KF):
                    through(w0_t[:, k, :], vec0[:, t, :], wa0[:, k, t:t + 1])
                    for h in range(H):
                        cols = slice(h * D, (h + 1) * D)
                        through(w1_t[:, k, cols], vec1[:, t, cols], wa1[:, k, t * H + h:t * H + h + 1])
                for k in range(KH):
                    through(w2_t[:, k, :], vec2[:, t, :], wa2[:, k, t:t + 1])
            for k in range(KF):
                const(nc.vector.tensor_scalar(wa0_wide[:, k, :], ones[:], wa0[:, k, 0:1], None, ALU.mult))
            assert count[0] == VECTOR_CONSTS, count[0]

            sa = Steps(dve, a_steps, A_STEPS)
            sbc = Steps(dve, b_steps, B_STEPS)

            def gate(slot):
                nc.vector.memset(gate_t[:, slot:slot + 1], 0.0)

            def moments_of(st, src, stats_t, moments_t, var_t, var_sem):
                for b in range(NB):
                    st.done(nc.vector.bn_stats(stats_t[:, b, :], src[:, b, :]))
                st.wait()
                gate(6 if st is sa else 7)
                for b in range(NB):
                    st.done(nc.vector.bn_aggr(moments_t[:, b, :], stats_t[:, b, :]))
                st.wait()
                nc.vector.tensor_scalar(var_t[:], moments_t[:, :, 1], EPS, None, ALU.add).then_inc(var_sem, 1)

            def normed(g, src, moments_t, rstd_t, rstd_sem, dst, ready):
                dve.wait_ge(rstd_sem, nth(1, g, 0))
                for b in range(NB):
                    last = nc.vector.tensor_scalar(dst[:, b, :], src[:, b, :], moments_t[:, b, 0:1],
                                                   rstd_t[:, b:b + 1], ALU.subtract, ALU.mult)
                last.then_inc(ready, 1)

            def stage_a(g, p, piece):
                first = isinstance(g, int) and g == 0
                reused = not (isinstance(g, int) and g < 2)
                if piece == 0:
                    sa.begin(g)
                    dve.wait_ge(adj_in[p], 16 * (g // 2 + 1) if isinstance(g, int) else 8 * (g + (2 - p)))
                    if reused:
                        dve.wait_ge(masked_ready, nth(10, g - 2, 9))
                    nc.vector.tensor_scalar(mask[p][:], adj_t[p][:], 0.0, NO_EDGE, ALU.is_le,
                                            ALU.mult).then_inc(mask_ready, 1)
                    dve.wait_ge(a_full[1], nth(A_TURNS, g, A_X))
                    nc.vector.tensor_copy(xT[:, 1, :], bank_a[1][:]).then_inc(a_taken[1], 1)
                    dve.wait_ge(a_full[1], nth(A_TURNS, g, A_MASK))
                    nc.vector.tensor_copy(mask_T[p][:, 2:4, :], bank_a[1][:].bitcast(BF16)
                                          .rearrange("p (b n) -> p b n", b=2)).then_inc(a_taken[1], 1)
                if piece == 1:
                    dve.wait_ge(a_full[0], nth(A_TURNS, g, A_LOGIT))
                    sa.done(nc.vector.tensor_copy(sj[:, 0, :], bank_a[0][:, 0:NB]))
                    nc.vector.tensor_scalar(sj[:, 1, :], bank_a[0][:, 0:NB], SLOPE, None,
                                            ALU.mult).then_inc(a_taken[0], 1)
                    sa.wait()
                    dve.wait_ge(low0_ready, nth(1, g, 0))
                    for b in range(NB):
                        last = nc.vector.scalar_tensor_tensor(out=edge0[:, b, :], in0=bank_a[1][:],
                                                              scalar=sj[:, 0, b:b + 1], in1=edge0[:, b, :],
                                                              op0=ALU.add, op1=ALU.max)
                    last.then_inc(a_taken[1], 1)
                    dve.wait_ge(a_taken[0], nth(A_TURNS, g, A_MASK))
                    dve.wait_ge(a_taken[1], nth(A_TURNS, g, A_LOGIT))
                    gate(5)
                    for b in range(NB):
                        sa.done(nc.vector.tensor_tensor_reduce(edge0[:, b, :], edge0[:, b, :],
                                                               mask_T[p][:, b, :], 1.0, LOWEST, ALU.add,
                                                               ALU.max, top0[:, b:b + 1]))
                    sa.wait()
                    nc.vector.tensor_scalar(neg_top0[:], top0[:], -1.0, None,
                                            ALU.mult).then_inc(masked0_ready, 1)
                if piece == 2:
                    dve.wait_ge(prob0_ready, nth(1, g, 0))
                    nc.vector.reciprocal(rden0[:], den0[:]).then_inc(rden0_ready, 1)
                if piece == 3:
                    dve.wait_ge(a_taken[0], nth(A_TURNS, g, A_OUT))
                    dve.wait_ge(a_taken[1], nth(A_TURNS, g, A_OUT))
                    nc.vector.scalar_tensor_tensor(out=leak0[:], in0=mix0[:], scalar=SLOPE, in1=mix0[:],
                                                   op0=ALU.mult, op1=ALU.max).then_inc(leak0_ready, 1)
                    dve.wait_ge(sum0_ready, nth(1, g, 0))
                    moments_of(sa, leak0, stats, moments, var_eps, var_ready)
                    normed(g, leak0, moments, rstd, rstd_ready, x1[p], x1_ready)
                    sa.end()

            def split(src, parts, n, ready):
                r = rest[:, :, 0:n]
                sbc.done(nc.vector.tensor_copy(parts[:, :, 0:n], src))
                sbc.wait()
                sbc.done(nc.vector.tensor_tensor(r, src, parts[:, :, 0:n], ALU.subtract))
                sbc.wait()
                sbc.done(nc.vector.tensor_copy(parts[:, :, n:2 * n], r))
                sbc.wait()
                sbc.done(nc.vector.tensor_tensor(r, r, parts[:, :, n:2 * n], ALU.subtract))
                sbc.wait()
                nc.vector.tensor_copy(parts[:, :, 2 * n:3 * n], r).then_inc(ready, 1)

            def maxima(g, p, n, hn, turn, i):
                dve.wait_ge(row_full[i], nth(ROW_TURNS, g, turn))
                gate(n)
                for b in range(NB):
                    last = nc.vector.tensor_tensor_reduce(junk[:, i, b, :], bank_row[i][:], mask_T[p][:, b, :], 1.0,
                                                          LOWEST, ALU.add, ALU.max, top[:, b, hn:hn + 1])
                last.then_inc(row_taken[i], 1)

            def shifts(b_cols, n, parts, ready):
                t, c = top[:, :, 0:n], shift[:, :, 0:n]
                sbc.done(nc.vector.tensor_tensor(t, t, b_cols, ALU.add))
                sbc.wait()
                sbc.done(nc.vector.scalar_tensor_tensor(out=c, in0=t, scalar=SLOPE, in1=t, op0=ALU.mult,
                                                        op1=ALU.max))
                sbc.wait()
                sbc.done(nc.vector.tensor_tensor(v[:, :, 0:n], b_cols, c, ALU.subtract))
                sbc.done(nc.vector.scalar_tensor_tensor(out=v[:, :, n:2 * n], in0=b_cols, scalar=SLOPE,
                                                        in1=c, op0=ALU.mult, op1=ALU.subtract))
                sbc.wait()
                split(v[:, :, 0:2 * n], parts, 2 * n, ready)

            def joined(g, n, turn, i, a_of):
                dve.wait_ge(row_full[i], nth(ROW_TURNS, g, turn))
                dve.wait_ge(low_ready, nth(5, g, n))
                t = logit[n % 2]
                for b in range(NB):
                    last = nc.vector.scalar_tensor_tensor(out=t[:, b, :], in0=bank_row[i][:], scalar=a_of(b),
                                                          in1=t[:, b, :], op0=ALU.add, op1=ALU.max)
                last.then_inc(row_taken[i], 1)

            def denominators(g, n):
                for i in range(2):
                    dve.wait_ge(o_full[i], nth(O_TURNS, g, B_HEADS + n))
                    if n:
                        dve.wait_ge(o_taken[i], nth(O_TURNS, g, B_HEADS + n - 1))
                    den = bank_o[i][:, 0:2 * (D + 1)].rearrange("p (b f) -> p b f", b=2)[:, :, D]
                    nc.vector.reciprocal(rden[:, 2 * i:2 * i + 2], den).then_inc(rden_ready, 1)

            def stage_bc(g, p, stage_a):
                sbc.begin(g)
                dve.wait_ge(o_full[1], nth(O_TURNS, g, B_X1T))
                nc.vector.tensor_copy(x1T[:, 1, :], bank_o[1][:]).then_inc(o_taken[1], 1)
                dve.wait_ge(small_full, nth(SMALL_TURNS, g, COLS1))
                nc.vector.tensor_copy(ab[:], bank_small[:, 0:NB * 2 * H]
                                      .rearrange("p (b c) -> p b c", b=NB)).then_inc(small_taken, 1)
                dve.wait_ge(small_taken, nth(SMALL_TURNS, g, COLS1))
                nc.vector.tensor_scalar(a_low[:], ab[:, :, 0:H], SLOPE, None, ALU.mult).then_inc(a_low_ready, 1)
                split(ab[:, :, 0:H], a_parts, H, parts_ready)
                dve.wait_ge(small_full, nth(SMALL_TURNS, g, AROW1))
                nc.vector.tensor_copy(a_rows[:], bank_small[0:3 * H, 0:N // 2].bitcast(BF16)).then_inc(small_taken, 1)
                dve.wait_ge(self_edges, nth(1, g, 0))
                for n in range(H):
                    maxima(g, p, n, n, n // 2, n % 2)
                dve.wait_ge(row_taken[1], nth(ROW_TURNS, g, 1))
                shifts(ab[:, :, H:2 * H], H, v_parts, parts_ready)
                dve.wait_ge(small_full, nth(SMALL_TURNS, g, VROW1))
                nc.vector.tensor_copy(v_rows[:], bank_small[0:6 * H, 0:N // 2].bitcast(BF16)).then_inc(small_taken, 1)
                if stage_a:
                    stage_a(g + 1, 1 - p, 0)
                for n in range(H):
                    joined(g, n, 2 + n // 2, n % 2, lambda b: ab[:, b, n:n + 1])
                    if n >= 2:
                        denominators(g, n - 2)
                if stage_a:
                    stage_a(g + 1, 1 - p, 1)
                denominators(g, 2)
                denominators(g, 3)
                dve.wait_ge(exp_h_ready, nth(1, g, 0))
                sbc.done(nc.vector.tensor_scalar(hid[:], hid[:], 0.0, -1.0, ALU.max, ALU.add))
                sbc.wait()
                nc.vector.scalar_tensor_tensor(out=hid[:], in0=logit[1][:], scalar=1.0, in1=hid[:],
                                               op0=ALU.min, op1=ALU.add).then_inc(hid_ready, 1)
                for k in range(1, KH, 2):
                    dve.wait_ge(o_full[1], nth(O_TURNS, g, B_HT + k // 2))
                    nc.vector.tensor_copy(hid_T[:, k, :], bank_o[1][:]).then_inc(o_taken[1], 1)
                if stage_a:
                    stage_a(g + 1, 1 - p, 2)
                dve.wait_ge(small_full, nth(SMALL_TURNS, g, COLS2))
                nc.vector.tensor_copy(ab2[:], bank_small[:, 0:NB * 2]
                                      .rearrange("p (b c) -> p b c", b=NB)).then_inc(small_taken, 1)
                dve.wait_ge(small_taken, nth(SMALL_TURNS, g, COLS2))
                nc.vector.tensor_scalar(a2_low[:], ab2[:, :, 0:1], SLOPE, None, ALU.mult).then_inc(a_low_ready, 1)
                split(ab2[:, :, 0:1], a2_parts, 1, parts_ready)
                dve.wait_ge(small_full, nth(SMALL_TURNS, g, AROW2))
                nc.vector.tensor_copy(a2_rows[:], bank_small[0:3, 0:N // 2].bitcast(BF16)).then_inc(small_taken, 1)
                maxima(g, p, 4, 0, 4, 0)
                dve.wait_ge(row_taken[0], nth(ROW_TURNS, g, 4))
                shifts(ab2[:, :, 1:2], 1, v2_parts, parts_ready)
                dve.wait_ge(small_full, nth(SMALL_TURNS, g, VROW2))
                nc.vector.tensor_copy(v2_rows[:], bank_small[0:6, 0:N // 2].bitcast(BF16)).then_inc(small_taken, 1)
                joined(g, 4, 4, 1, lambda b: ab2[:, b, 0:1])
                for b in range(NB):
                    i = b % 2
                    dve.wait_ge(o_full[i], nth(O_TURNS, g, C_OUT + b // 2))
                    sbc.done(nc.vector.reciprocal(rden[:, b:b + 1], bank_o[i][:, F:F + 1]))
                    sbc.wait()
                    nc.vector.scalar_tensor_tensor(out=y2[:, b, :], in0=bank_o[i][:, 0:F],
                                                   scalar=rden[:, b:b + 1], in1=x1[p][:, b, :],
                                                   op0=ALU.mult, op1=ALU.add).then_inc(o_taken[i], 1)
                for i in range(2):
                    dve.wait_ge(o_taken[i], nth(O_TURNS, g, C_OUT + 1))
                moments_of(sbc, y2, stats2, moments2, var_eps2, var2_ready)
                if not (isinstance(g, int) and g == 0):
                    dve.wait_ge(out_stored[1 - p], 16 * ((g + 1) // 2) if isinstance(g, int)
                                else 8 * (g + p))
                normed(g, y2, moments2, rstd2, rstd2_ready, out_t, out_ready)
                sbc.end()
                if stage_a:
                    stage_a(g + 1, 1 - p, 3)

            schedule(dve, stage_a, stage_bc)

        @block.tensor
        def _(pe):
            pe.wait_ge(pool_consts, POOL_CONSTS)
            pe.wait_ge(vector_consts, VECTOR_CONSTS)
            pe.wait_ge(weights_in, WEIGHTS)
            pe.wait_ge(bias3_in, 3 * 16)

            def taken(sems, i, turns, g, turn):
                if turn:
                    pe.wait_ge(sems[i], nth(turns, g, turn - 1))
                elif not (isinstance(g, int) and g == 0):
                    pe.wait_ge(sems[i], nth(turns, g - 1, turns - 1))

            def stage_a(g, p, piece):
                if piece == 0:
                    pe.wait_ge(x_in[p], 16 * (g // 2 + 1) if isinstance(g, int) else 8 * (g + (2 - p)))
                    for k in range(KF):
                        taken(a_taken, k, A_TURNS, g, A_X)
                        for b in range(NB):
                            last = nc.tensor.transpose(bank_a[k][:, b * P:(b + 1) * P],
                                                       x_t[p][:, b, k * P:(k + 1) * P], ident[:])
                        last.then_inc(a_full[k], 1)
                    pe.wait_ge(mask_ready, nth(1, g, 0))
                    for i in range(2):
                        taken(a_taken, i, A_TURNS, g, A_MASK)
                        rows = bank_a[i][:].bitcast(BF16).rearrange("p (b n) -> p b n", b=2)
                        for j in range(2):
                            for b in range(NB):
                                d = 2 * i + j
                                last = nc.tensor.transpose(rows[:, j, b * P:(b + 1) * P],
                                                           mask[p][:, b, d * P:(d + 1) * P], ident_b[:])
                        last.then_inc(a_full[i], 1)
                if piece == 1:
                    taken(a_taken, 0, A_TURNS, g, A_LOGIT)
                    taken(a_taken, 1, A_TURNS, g, A_LOGIT)
                    for b in range(NB):
                        for k in range(KF):
                            last = nc.tensor.matmul(bank_a[0][:, b:b + 1], xT[:, k, b * P:(b + 1) * P],
                                                    wa0[:, k, 1:2], start=(k == 0), stop=(k == KF - 1))
                    last.then_inc(a_full[0], 1)
                    for k in range(KF):
                        last = nc.tensor.matmul(bank_a[1][:], wa0_wide[:, k, :], xT[:, k, :],
                                                start=(k == 0), stop=(k == KF - 1))
                    last.then_inc(a_full[1], 1)
                if piece == 2:
                    for i in range(2):
                        pe.wait_ge(a_taken[i], nth(A_TURNS, g, A_LOGIT))
                    for b in range(NB):
                        for k in range(KF):
                            last = nc.tensor.matmul(bank_a[b // 2][:, (b % 2) * F:(b % 2 + 1) * F],
                                                    xT[:, k, b * P:(b + 1) * P], w0_t[:, k, :],
                                                    start=(k == 0), stop=(k == KF - 1))
                        if b % 2:
                            last.then_inc(a_full[b // 2], 1)
                if piece == 3:
                    pe.wait_ge(prob0_ready, nth(1, g, 0))
                    for i in range(2):
                        pe.wait_ge(a_taken[i], nth(A_TURNS, g, A_VALUES))
                    for b in range(NB):
                        for k in range(NB):
                            last = nc.tensor.matmul(bank_a[b // 2][:, (b % 2) * F:(b % 2 + 1) * F],
                                                    weight0[:, k, b * P:(b + 1) * P], values0[:, k, :],
                                                    start=(k == 0), stop=(k == NB - 1))
                        if b % 2:
                            last.then_inc(a_full[b // 2], 1)

            def small(g, turn, ready, parts, n):
                pe.wait_ge(parts_ready, nth(4, g, ready))
                pe.wait_ge(small_taken, nth(SMALL_TURNS, g, turn - 1))
                rows = bank_small[0:n, 0:N // 2].bitcast(BF16)
                for b in range(NB):
                    last = nc.tensor.transpose(rows[:, b * P:(b + 1) * P], parts[:, b, :], ident_b[:])
                last.then_inc(small_full, 1)

            def row(g, i, turn, pick, q, rows):
                taken(row_taken, i, ROW_TURNS, g, turn)
                nc.tensor.matmul(bank_row[i][:], pick[:, q, :], rows[:], start=True,
                                 stop=True).then_inc(row_full[i], 1)

            def stage_bc(g, p, stage_a):
                first = isinstance(g, int) and g == 0
                pe.wait_ge(x1_ready, nth(1, g, 0))
                for k in range(KF):
                    taken(o_taken, k, O_TURNS, g, B_X1T)
                    for b in range(NB):
                        last = nc.tensor.transpose(bank_o[k][:, b * P:(b + 1) * P],
                                                   x1[p][:, b, k * P:(k + 1) * P], ident[:])
                    last.then_inc(o_full[k], 1)
                for k in range(KF):
                    pe.wait_ge(o_taken[k], nth(O_TURNS, g, B_X1T))
                if not first:
                    pe.wait_ge(small_taken, nth(SMALL_TURNS, g - 1, VROW2))
                for b in range(NB):
                    for k in range(KF):
                        last = nc.tensor.matmul(bank_small[:, b * 2 * H:(b + 1) * 2 * H],
                                                x1T[:, k, b * P:(b + 1) * P], wa1[:, k, :],
                                                start=(k == 0), stop=(k == KF - 1))
                last.then_inc(small_full, 1)
                for b in range(NB):
                    taken(o_taken, b % 2, O_TURNS, g, B_XL + b // 2)
                    nc.tensor.matmul(bank_o[b % 2][:], ones3[:], bias3[:, 0:HD], start=True, stop=False)
                    for k in range(KF):
                        last = nc.tensor.matmul(bank_o[b % 2][:], x1T[:, k, b * P:(b + 1) * P], w1_t[:, k, :],
                                                start=False, stop=(k == KF - 1))
                    last.then_inc(o_full[b % 2], 1)
                small(g, AROW1, 0, a_parts, 3 * H)
                pe.wait_ge(small_taken, nth(SMALL_TURNS, g, AROW1))
                for n in range(H):
                    row(g, n % 2, n // 2, pick_a1, n, a_rows)
                small(g, VROW1, 1, v_parts, 6 * H)
                if stage_a:
                    stage_a(g + 1, 1 - p, 0)

                def logit_rows(n, pick, q, rows, turn, i):
                    row(g, i, turn, pick, q, rows)
                    if n:
                        pe.wait_ge(low_ready, nth(5, g, n - 1))
                    elif not first:
                        pe.wait_ge(low_ready, nth(5, g - 1, 4))
                    if n >= 2:
                        pe.wait_ge(prob_ready, nth(5, g, n - 2))
                    elif not first:
                        pe.wait_ge(prob_ready, nth(5, g - 1, 4))
                    nc.tensor.matmul(bank_v2[:], pick[:, q + pick.shape[1] // 2, :], rows[:], start=True,
                                     stop=True).then_inc(v2_full, 1)

                def rows1(n):
                    logit_rows(n, pick_v1, n, v_rows, 2 + n // 2, n % 2)

                def head(n):
                    pe.wait_ge(prob_ready, nth(5, g, n))
                    for b in range(NB):
                        i = b // 2
                        if b % 2 == 0:
                            taken(o_taken, i, O_TURNS, g, B_HEADS + n)
                        for k in range(NB):
                            last = nc.tensor.matmul(bank_o[i][:, (b % 2) * (D + 1):(b % 2 + 1) * (D + 1)],
                                                    prob[n % 2][:, k, b * P:(b + 1) * P], xl1[:, k, n, :],
                                                    start=(k == 0), stop=(k == NB - 1))
                        if b == 1:
                            last.then_inc(o_full[0], 1)
                        if b == NB - 1:
                            last.then_inc(o_full[1], 1)

                pe.wait_ge(small_taken, nth(SMALL_TURNS, g, VROW1))
                rows1(0)
                rows1(1)
                head(0)
                rows1(2)
                head(1)
                rows1(3)
                head(2)
                if stage_a:
                    stage_a(g + 1, 1 - p, 1)
                head(3)
                pe.wait_ge(hid_ready, nth(1, g, 0))
                for k in range(KH):
                    taken(o_taken, k % 2, O_TURNS, g, B_HT + k // 2)
                    for b in range(NB):
                        last = nc.tensor.transpose(bank_o[k % 2][:, b * P:(b + 1) * P],
                                                   hid[:, b, k * P:(k + 1) * P], ident[:])
                    last.then_inc(o_full[k % 2], 1)
                if stage_a:
                    stage_a(g + 1, 1 - p, 2)
                for i in range(2):
                    pe.wait_ge(o_taken[i], nth(O_TURNS, g, B_HT + 1))
                for b in range(NB):
                    for k in range(KH):
                        last = nc.tensor.matmul(bank_small[:, b * 2:(b + 1) * 2],
                                                hid_T[:, k, b * P:(b + 1) * P], wa2[:, k, :],
                                                start=(k == 0), stop=(k == KH - 1))
                last.then_inc(small_full, 1)
                for b in range(NB):
                    cols = bank_o[b // 2][:, (b % 2) * F:(b % 2 + 1) * F]
                    nc.tensor.matmul(cols, ones3[:], bias3[:, HD:HD + F], start=True, stop=False)
                    for k in range(KH):
                        last = nc.tensor.matmul(cols, hid_T[:, k, b * P:(b + 1) * P], w2_t[:, k, :],
                                                start=False, stop=(k == KH - 1))
                    if b % 2:
                        last.then_inc(o_full[b // 2], 1)
                small(g, AROW2, 2, a2_parts, 3)
                pe.wait_ge(small_taken, nth(SMALL_TURNS, g, AROW2))
                row(g, 0, 4, pick_a2, 0, a2_rows)
                small(g, VROW2, 3, v2_parts, 6)
                pe.wait_ge(small_taken, nth(SMALL_TURNS, g, VROW2))
                logit_rows(4, pick_v2, 0, v2_rows, 4, 1)
                if stage_a:
                    stage_a(g + 1, 1 - p, 3)
                pe.wait_ge(prob_ready, nth(5, g, 4))
                for b in range(NB):
                    i = b % 2
                    taken(o_taken, i, O_TURNS, g, C_OUT + b // 2)
                    for k in range(NB):
                        last = nc.tensor.matmul(bank_o[i][:, 0:F + 1], prob[0][:, k, b * P:(b + 1) * P],
                                                xl2[:, k, :], start=(k == 0), stop=(k == NB - 1))
                    last.then_inc(o_full[i], 1)

            schedule(pe, stage_a, stage_bc)


_INS = ['x', 'adj', 'L0_gnn_W', 'L0_gnn_a', 'L1_gnn_W1', 'L1_gnn_att_src1', 'L1_gnn_att_dst1', 'L1_gnn_b1',
        'L1_gnn_W2', 'L1_gnn_att_src2', 'L1_gnn_att_dst2', 'L1_gnn_b2']


def kernel(**inputs):
    import numpy as _np
    import concourse.bacc as _bacc
    from concourse.bass_utils import run_bass_kernel_spmd as _run

    nc = _bacc.Bacc("TRN2", target_bir_lowering=False, num_devices=1)
    arrays, args = {}, []
    for name in _INS:
        a = _np.ascontiguousarray(inputs[name])
        arrays[f"in_{name}_dram"] = a
        args.append(nc.dram_tensor(f"in_{name}_dram", a.shape, mybir.dt.from_np(a.dtype), kind="ExternalInput").ap())
    args.append(nc.dram_tensor("out_0_dram", inputs['x'].shape, F32, kind="ExternalOutput").ap())
    build(nc, *args)
    r = _run(nc, [arrays], core_ids=[0])
    return r.results[0]["out_0_dram"]
```

```python
from contextlib import ExitStack

import concourse.bass as bass
from concourse import mybir

F32 = mybir.dt.float32
BF16 = mybir.dt.bfloat16
I32 = mybir.dt.int32
ALU = mybir.AluOpType
ACT = mybir.ActivationFunctionType

P = 128
SLOPE = 0.2
EPS = 1e-5
NO_EDGE = -9.0e15
LOWEST = -3.0e38

A_X, A_MASK, A_LOGIT, A_VALUES, A_OUT, A_X1T, A_TURNS = range(7)
C_HT, C_XL, B_XL, B_HEADS, C_OUT = 0, 2, 4, (6, 7, 8, 9), (10, 11)
COLS1, AROW1, VROW1, AROW2, VROW2 = range(5)
PARTS_A1, PARTS_V1, PARTS_A2, PARTS_V2 = range(4)
HEAD_1, HEAD_2 = (0, 1, 2, 3), 4
ROW_A1 = [(0, 0), (1, 0), (0, 1), (1, 1)]
ROW_V1 = [(1, 2), (0, 3), (1, 3), (0, 4)]
ROW_A2, ROW_V2 = (0, 2), (1, 4)
A_STEPS, B_STEPS, C_STEPS, N_STEPS = 13, 12, 12, 8


def nth(per_graph, g, k):
    return g * per_graph + (k + 1)


class Turns:

    def __init__(self, owners, steps):
        self.owners, self.steps = owners, steps

    def before(self, step, k):
        n = step * len(self.owners) + k
        if isinstance(step, int) and step == 0:
            return n - self.owners[:k].count("C")
        if isinstance(step, int) and step == self.steps:
            n = n - self.owners[:k].count("B")
        return n - self.owners.count("C")

    def done(self, step, k):
        return self.before(step, k) + 1


class Steps:

    def __init__(self, engine, semaphore, per_graph):
        self.engine, self.semaphore, self.per_graph = engine, semaphore, per_graph

    def begin(self, g):
        self.g, self.k = g, 0

    def resume(self, g):
        self.g = g

    def done(self, instruction):
        instruction.then_inc(self.semaphore, 1)
        self.k += 1

    def wait(self):
        self.engine.wait_ge(self.semaphore, nth(self.per_graph, self.g, self.k - 1))

    def end(self):
        assert self.k == self.per_graph, (self.semaphore, self.k)


def build(nc, x, adj, w0, a0, w1, src1, dst1, b1, w2, src2, dst2, b2, out):
    G, N, F = x.shape
    NB = N // P
    KF = F // P
    H = src1.shape[0]
    D = src1.shape[1]
    HD = H * D
    KH = HD // P
    assert N == 512 and D == P and F == 256 and H == 4 and G % 2 == 0

    with ExitStack() as ctx:
        def sb(name, shape, dt=F32):
            return ctx.enter_context(nc.sbuf_tensor(name, shape, dt))

        def bank(name):
            return ctx.enter_context(nc.psum_tensor(name, [P, 512], F32))

        def sem(name):
            return ctx.enter_context(nc.semaphore(name))

        ident = sb("ident", [P, P])
        ident_b = sb("ident_b", [P, P], BF16)
        off_diag = sb("off_diag", [P, P], BF16)
        ones = sb("ones", [P, P])
        pick_a1 = sb("pick_a1", [3 * H, H, P], BF16)
        pick_v1 = sb("pick_v1", [6 * H, 2 * H, P], BF16)
        pick_a2 = sb("pick_a2", [3, 1, P], BF16)
        pick_v2 = sb("pick_v2", [6, 2, P], BF16)
        w0_t = sb("w0_t", [P, KF, F])
        w1_t = sb("w1_t", [P, KF, HD])
        w2_t = sb("w2_t", [P, KH, 2 + F])
        wa0 = sb("wa0", [P, KF, 2])
        wa1 = sb("wa1", [P, KF, 2 * H])
        wa0_wide = sb("wa0_wide", [P, KF, P])
        bias_parts = sb("bias_parts", [1, 3, HD + 2 + F], BF16)
        bias3 = sb("bias3", [3, HD + 2 + F], BF16)
        ones3 = sb("ones3", [3, P], BF16)
        minus_half = sb("minus_half", [P, NB])
        gate_t = sb("gate_t", [P, 9])

        x_t = sb("x_t", [P, NB, F])
        adj_t = sb("adj_t", [P, NB, N], I32)
        mask = [sb(f"mask{i}", [P, NB, N], BF16) for i in range(3)]
        mask_T = [sb(f"mask_T{i}", [P, NB, N], BF16) for i in range(3)]
        x1 = [sb(f"x1_{i}", [P, NB, F]) for i in range(3)]
        xT = sb("xT", [P, KF, N])
        sj = sb("sj", [P, 2, NB])
        logit0 = sb("logit0", [P, NB, N])
        prob0 = sb("prob0", [P, NB, N])
        top0 = sb("top0", [P, NB])
        neg_top0 = sb("neg_top0", [P, NB])
        den0 = sb("den0", [P, NB])
        rden0 = sb("rden0", [P, NB])
        values0 = sb("values0", [P, NB, F])
        mix0 = sb("mix0", [P, NB, F])
        leak0 = sb("leak0", [P, NB, F])
        stats = sb("stats", [P, NB, 6])
        moments = sb("moments", [P, NB, 2])
        var_eps = sb("var_eps", [P, NB])
        rstd = sb("rstd", [P, NB])
        x1T = sb("x1T", [P, KF, N])
        ab = sb("ab", [P, NB, 2 * H])
        a_low = sb("a_low", [P, NB, H])
        a2_low = sb("a2_low", [P, NB, 1])
        rest = sb("rest", [P, NB, 2 * H])
        a_parts = sb("a_parts", [P, NB, 3 * H], BF16)
        v_parts = sb("v_parts", [P, NB, 6 * H], BF16)
        a2_parts = sb("a2_parts", [P, NB, 3], BF16)
        v2_parts = sb("v2_parts", [P, NB, 6], BF16)
        a_rows = sb("a_rows", [3 * H, N], BF16)
        v_rows = sb("v_rows", [6 * H, N], BF16)
        a2_rows = sb("a2_rows", [3, N], BF16)
        v2_rows = sb("v2_rows", [6, N], BF16)
        top = sb("top", [P, NB, H])
        shift = sb("shift", [P, NB, H])
        v = sb("v", [P, NB, 2 * H])
        rest2 = sb("rest2", [P, NB, 2])
        top2 = sb("top2", [P, NB, 1])
        shift2 = sb("shift2", [P, NB, 1])
        v_2 = sb("v_2", [P, NB, 2])
        rden2 = sb("rden2", [P, NB])
        junk = sb("junk", [P, 2, NB, N], BF16)
        logit2 = sb("logit2", [P, NB, N])
        prob2 = sb("prob2", [P, NB, N])
        xl1 = sb("xl1", [P, NB, H, D + 1])
        xl2 = sb("xl2", [P, NB, 2 + F + 1])
        logit = [sb(f"logit1_{i}", [P, NB, N]) for i in range(2)]
        prob = [sb(f"prob1_{i}", [P, NB, N]) for i in range(2)]
        rden = sb("rden", [P, NB])
        hid = sb("hid", [P, NB, HD])
        hid_line = hid[0:1, :, :].rearrange("p b n -> p (b n)")
        bias_row = hid_line[:, 0:HD + 2 + F]
        bias_rest = hid_line[:, HD + 2 + F:2 * (HD + 2 + F)]
        hid_T = sb("hid_T", [P, KH, N])
        vec1 = hid_T[:, 0:2, :]
        vec0 = hid_T[:, 2, :].rearrange("p (t f) -> p t f", t=2)
        vec2 = hid_T[:, 3, :].rearrange("p (t f) -> p t f", t=2)
        scratch = x1T[:, 0, :]
        y2 = sb("y2", [P, NB, F])
        stats2 = sb("stats2", [P, NB, 6])
        moments2 = sb("moments2", [P, NB, 2])
        var_eps2 = sb("var_eps2", [P, NB])
        rstd2 = sb("rstd2", [P, NB])
        out_t = sb("out_t", [P, NB, F])

        bank_a = [bank(f"bank_a{i}") for i in range(2)]
        bank_small = bank("bank_small")
        bank_row = [bank(f"bank_row{i}") for i in range(2)]
        bank_v2 = bank("bank_v2")
        bank_o = [bank(f"bank_o{i}") for i in range(2)]

        a_full = [sem(f"a_full{i}") for i in range(2)]
        a_taken = [sem(f"a_taken{i}") for i in range(2)]
        small_full, small_taken = sem("small_full"), sem("small_taken")
        row_full = [sem(f"row_full{i}") for i in range(2)]
        row_taken = [sem(f"row_taken{i}") for i in range(2)]
        v2_full, v2_taken = sem("v2_full"), sem("v2_taken")
        o_full = [sem(f"o_full{i}") for i in range(2)]
        o_taken = [sem(f"o_taken{i}") for i in range(2)]

        weights_in = sem("weights_in")
        bias_parts_ready = sem("bias_parts_ready")
        bias3_in = sem("bias3_in")
        pool_consts = sem("pool_consts")
        vector_consts = sem("vector_consts")
        x_in = sem("x_in")
        adj_in = sem("adj_in")
        out_stored = sem("out_stored")
        mask_ready = sem("mask_ready")
        self_edges = sem("self_edges")
        low0_ready = sem("low0_ready")
        masked0_ready = sem("masked0_ready")
        prob0_ready = sem("prob0_ready")
        rden0_ready = sem("rden0_ready")
        leak0_ready = sem("leak0_ready")
        sum0_ready = sem("sum0_ready")
        var_ready = sem("var_ready")
        rstd_ready = sem("rstd_ready")
        x1_ready = sem("x1_ready")
        a_steps = sem("a_steps")
        b_steps = sem("b_steps")
        n_steps = sem("n_steps")
        c_steps = sem("c_steps")
        parts_ready = sem("parts_ready")
        a_low_ready = sem("a_low_ready")
        low_ready = sem("low_ready")
        masked_ready = sem("masked_ready")
        prob_ready = sem("prob_ready")
        rden_ready = sem("rden_ready")
        exp_h_ready = sem("exp_h_ready")
        elu_high_ready = sem("elu_high_ready")
        hid_ready = sem("hid_ready")
        rden2_ready = sem("rden2_ready")
        sum2_ready = sem("sum2_ready")
        var2_ready = sem("var2_ready")
        rstd2_ready = sem("rstd2_ready")
        out_ready = sem("out_ready")

        POOL_CONSTS, VECTOR_CONSTS = 26, 5 + 2 * (KF * (1 + H) + KH) + KF
        WEIGHTS = 8 * 16

        block = ctx.enter_context(nc.Block())

        o_turn = Turns("CCCCBBBBBBCC", G)
        small_turn = Turns("BBBCC", G)
        row_turn = [Turns("BBCBB", G), Turns("BBBBC", G)]
        head_turn = Turns("BBBBC", G)
        half_turn = Turns("BBBBBBBBCC", G)
        parts_turn = Turns("BBCC", G)
        layer_turn = Turns("BC", G)

        def schedule(engine, stage_a, step, finish):
            for piece in range(8):
                stage_a(0, 0, piece)
            step(0, 0, True, True, False)
            step(1, 1, True, True, True)
            step(2, 2, True, True, True)
            assert (G - 4) % 3 == 0
            with engine.Fori(3, G - 1, 3) as i:
                for r in range(3):
                    step(i + r, r, True, True, True)
            step(G - 1, (G - 1) % 3, False, True, True)
            step(G, G % 3, False, False, True)
            finish(G - 1)

        def tail_of(step):
            return not (isinstance(step, int) and step < 2)

        @block.sync
        def _(sp):
            for tile, src in (
                (w0_t[:], w0.rearrange("(k p) n -> p k n", p=P)),
                (w1_t[:], w1.rearrange("(k p) n -> p k n", p=P)),
                (w2_t[:, :, 2:], w2.rearrange("(k p) n -> p k n", p=P)),
                (vec0, a0.rearrange("(a t f) o -> a t (f o)", a=1, t=2).broadcast_to([P, 2, F])),
                (vec1[:, 0, :], src1.rearrange("(a h) f -> a (h f)", a=1).broadcast_to([P, HD])),
                (vec1[:, 1, :], dst1.rearrange("(a h) f -> a (h f)", a=1).broadcast_to([P, HD])),
                (vec2[:, 0, :], src2.broadcast_to([P, F])),
                (vec2[:, 1, :], dst2.broadcast_to([P, F])),
            ):
                sp.dma_start(tile, src).then_inc(weights_in, 16)
            sp.dma_start(bias_row[:, 0:HD], b1.rearrange("(a f) -> a f", a=1)).then_inc(bias3_in, 16)
            sp.dma_start(bias_row[:, HD + 2:], b2.rearrange("(a f) -> a f", a=1)).then_inc(bias3_in, 16)

            def load(g, reused=True):
                if reused:
                    sp.wait_ge(mask_ready, nth(1, g - 1, 0))
                sp.dma_start(adj_t[:], adj[g].rearrange("(b p) n -> p b n", p=P)).then_inc(adj_in, 16)
                if reused:
                    sp.wait_ge(sum0_ready, nth(1, g - 1, 0))
                sp.dma_start(x_t[:], x[g].rearrange("(b p) n -> p b n", p=P)).then_inc(x_in, 16)

            def store(g):
                sp.wait_ge(out_ready, nth(1, g, 0))
                sp.dma_start(out[g].rearrange("(b p) n -> p b n", p=P), out_t[:]).then_inc(out_stored, 16)

            load(0, False)
            sp.wait_ge(bias_parts_ready, 1)
            sp.dma_start(bias3[:], bias_parts[:]).then_inc(bias3_in, 16)
            load(1)
            load(2)
            load(3)
            with sp.Fori(4, G, 1) as i:
                store(i - 4)
                load(i)
            store(G - 4)
            store(G - 3)
            store(G - 2)
            store(G - 1)
            sp.wait_ge(out_stored, 16 * G)

        @block.gpsimd
        def _(pool):
            count = [0]

            def const(instruction):
                instruction.then_inc(pool_consts, 1)
                count[0] += 1
                pool.wait_ge(pool_consts, count[0])

            const(nc.gpsimd.memset(ones[:], 1.0))
            const(nc.gpsimd.memset(ones3[:], 1.0))
            const(nc.gpsimd.memset(minus_half[:], -0.5))
            const(nc.gpsimd.memset(xl1[:, :, :, D:D + 1], 1.0))
            const(nc.gpsimd.memset(xl2[:, :, 2 + F:], 1.0))
            const(nc.gpsimd.memset(ident[:], 0.0))
            const(nc.gpsimd.affine_select(out=ident[:], in_=ident[:], compare_op=ALU.not_equal, fill=1.0,
                                          base=0, pattern=[[-1, P]], channel_multiplier=1))
            const(nc.gpsimd.tensor_copy(ident_b[:], ident[:]))
            const(nc.gpsimd.memset(off_diag[:], 1.0))
            const(nc.gpsimd.affine_select(out=off_diag[:], in_=off_diag[:], compare_op=ALU.not_equal,
                                          fill=0.0, base=0, pattern=[[-1, P]], channel_multiplier=1))
            for pick, q in ((pick_a1, H), (pick_v1, 2 * H), (pick_a2, 1), (pick_v2, 2)):
                const(nc.gpsimd.memset(pick[:], 0.0))
                for part in range(3):
                    const(nc.gpsimd.affine_select(out=pick[:], in_=pick[:], compare_op=ALU.not_equal,
                                                  fill=1.0, base=-part * q, pattern=[[-1, q], [0, P]],
                                                  channel_multiplier=1))
            assert count[0] == POOL_CONSTS
            pool.wait_ge(vector_consts, VECTOR_CONSTS)

            def norm(g, var_sem, var, rstd_t, rstd_sem):
                pool.wait_ge(var_sem, nth(1, g, 0))
                nc.gpsimd.tensor_tensor(rstd_t[:], var[:], minus_half[:], ALU.pow).then_inc(rstd_sem, 1)

            def stage_a(g, slot, piece):
                if piece == 2:
                    pool.wait_ge(masked0_ready, nth(1, g, 0))
                    for m in (mask_T[slot], mask[slot]):
                        for b in range(NB):
                            d = m[:, b, b * P:(b + 1) * P]
                            last = nc.gpsimd.tensor_tensor(d, d, off_diag[:], ALU.mult)
                    last.then_inc(self_edges, 1)
                if piece == 4:
                    pool.wait_ge(leak0_ready, nth(1, g, 0))
                    nc.gpsimd.tensor_tensor(leak0[:], leak0[:], x_t[:], ALU.add).then_inc(sum0_ready, 1)
                    norm(g, var_ready, var_eps, rstd, rstd_ready)

            def masked(s, t, m, bank_at):
                i, turn = bank_at
                pool.wait_ge(row_taken[i], row_turn[i].done(s, turn))
                for half in range(2):
                    b = slice(half * NB // 2, (half + 1) * NB // 2)
                    nc.gpsimd.tensor_tensor(t[:, b, :], t[:, b, :], m[:, b, :], ALU.add).then_inc(masked_ready, 1)

            def tail(g):
                norm(g, var2_ready, var_eps2, rstd2, rstd2_ready)

            def step(s, slot, a, b, c):
                before, after = (slot + 2) % 3, (slot + 1) % 3
                if b:
                    masked(s, logit[0], mask[slot], ROW_V1[0])
                    masked(s, logit[1], mask[slot], ROW_V1[1])
                    masked(s, logit[0], mask[slot], ROW_V1[2])
                    masked(s, logit[1], mask[slot], ROW_V1[3])
                if c and tail_of(s):
                    tail(s - 2)
                if c:
                    masked(s, logit2, mask[before], ROW_V2)
                if a:
                    stage_a(s + 1, after, 4)
                    stage_a(s + 1, after, 2)
                if c:
                    for i in range(2):
                        pool.wait_ge(o_taken[i], o_turn.done(s, C_OUT[1]))
                    nc.gpsimd.tensor_tensor(y2[:], y2[:], x1[before][:], ALU.add).then_inc(sum2_ready, 1)

            schedule(pool, stage_a, step, tail)

        @block.scalar
        def _(act):
            act.wait_ge(vector_consts, VECTOR_CONSTS)
            act.wait_ge(pool_consts, POOL_CONSTS)

            def stage_a(g, slot, piece):
                if piece == 0:
                    for k in range(KF):
                        act.wait_ge(a_full[k], nth(A_TURNS, g, A_X))
                        nc.scalar.copy(xT[:, k, :], bank_a[k][:]).then_inc(a_taken[k], 1)
                    act.wait_ge(a_full[0], nth(A_TURNS, g, A_MASK))
                    nc.scalar.copy(mask_T[slot][:, 0:2, :], bank_a[0][:].bitcast(BF16)
                                   .rearrange("p (b n) -> p b n", b=2)).then_inc(a_taken[0], 1)
                if piece == 1:
                    act.wait_ge(a_full[1], nth(A_TURNS, g, A_LOGIT))
                    act.wait_ge(a_taken[0], nth(A_TURNS, g, A_LOGIT))
                    if not (isinstance(g, int) and g == 0):
                        act.wait_ge(prob0_ready, nth(1, g - 1, 0))
                    for b in range(NB):
                        last = nc.scalar.activation(logit0[:, b, :], bank_a[1][:], ACT.Identity,
                                                    bias=sj[:, 1, b:b + 1], scale=SLOPE)
                    last.then_inc(low0_ready, 1)
                if piece == 2:
                    act.wait_ge(masked0_ready, nth(1, g, 0))
                    for b in range(NB):
                        last = nc.scalar.activation(prob0[:, b, :], logit0[:, b, :], ACT.Exp,
                                                    bias=neg_top0[:, b:b + 1], accum_out=den0[:, b:b + 1])
                    last.then_inc(prob0_ready, 1)
                if piece == 3:
                    act.wait_ge(rden0_ready, nth(1, g, 0))
                    for b in range(NB):
                        if b % 2 == 0:
                            act.wait_ge(a_full[b // 2], nth(A_TURNS, g, A_VALUES))
                        last = nc.scalar.activation(values0[:, b, :], bank_a[b // 2][:, (b % 2) * F:(b % 2 + 1) * F],
                                                    ACT.Copy, scale=rden0[:, b:b + 1])
                        if b % 2:
                            last.then_inc(a_taken[b // 2], 1)
                if piece == 4:
                    for i in range(2):
                        act.wait_ge(a_full[i], nth(A_TURNS, g, A_OUT))
                        nc.scalar.copy(mix0[:, 2 * i:2 * i + 2, :], bank_a[i][:]
                                       .rearrange("p (b f) -> p b f", b=2)).then_inc(a_taken[i], 1)
                if piece == 5:
                    act.wait_ge(a_full[0], nth(A_TURNS, g, A_X1T))
                    nc.scalar.copy(x1T[:, 0, :], bank_a[0][:]).then_inc(a_taken[0], 1)

            def low(s, n, t, bias):
                act.wait_ge(v2_full, head_turn.done(s, n))
                act.wait_ge(a_low_ready, layer_turn.done(s, 1 if n == HEAD_2 else 0))
                for b in range(NB):
                    last = nc.scalar.activation(t[:, b, :], bank_v2[:], ACT.Identity, bias=bias(b))
                last.then_inc(low_ready, 1)

            def expo(s, n, dst, src):
                for half in range(2):
                    b = slice(half * NB // 2, (half + 1) * NB // 2)
                    act.wait_ge(masked_ready, half_turn.done(s, 2 * n + half))
                    last = nc.scalar.activation(dst[:, b, :], src[:, b, :], ACT.Exp)
                last.then_inc(prob_ready, 1)

            def take_head(s, n):
                for i in range(2):
                    act.wait_ge(rden_ready, nth(8, s, 2 * n + i))
                    for j in range(2):
                        b = 2 * i + j
                        last = nc.scalar.activation(hid[:, b, n * D:(n + 1) * D],
                                                    bank_o[i][:, j * (D + 1):j * (D + 1) + D],
                                                    ACT.Copy, scale=rden[:, b:b + 1])
                    last.then_inc(o_taken[i], 1)

            def step(s, slot, a, b, c):
                after = (slot + 1) % 3

                def take_xl1(q):
                    act.wait_ge(o_full[q % 2], o_turn.done(s, B_XL + q // 2))
                    nc.scalar.copy(xl1[:, q, :, 0:D], bank_o[q % 2][:]
                                   .rearrange("p (h f) -> p h f", h=H)).then_inc(o_taken[q % 2], 1)

                def low1(n):
                    if n >= 2:
                        act.wait_ge(prob_ready, head_turn.done(s, HEAD_1[n - 2]))
                    low(s, HEAD_1[n], logit[n % 2], lambda q: a_low[:, q, n:n + 1])

                def expo1(n):
                    if n >= 2:
                        act.wait_ge(o_full[1], o_turn.done(s, B_HEADS[n - 2]))
                    expo(s, HEAD_1[n], prob[n % 2], logit[n % 2])

                if c:
                    for k in range(KH):
                        act.wait_ge(o_full[k % 2], o_turn.done(s, C_HT + k // 2))
                        nc.scalar.copy(hid_T[:, k, :], bank_o[k % 2][:]).then_inc(o_taken[k % 2], 1)
                    for q in range(NB):
                        act.wait_ge(o_full[q % 2], o_turn.done(s, C_XL + q // 2))
                        nc.scalar.copy(xl2[:, q, 0:2 + F],
                                       bank_o[q % 2][:, 0:2 + F]).then_inc(o_taken[q % 2], 1)
                if a:
                    stage_a(s + 1, after, 0)
                if b:
                    low1(0)
                    low1(1)
                if a:
                    stage_a(s + 1, after, 1)
                if b:
                    take_xl1(0)
                    take_xl1(1)
                    expo1(0)
                    take_xl1(2)
                    low1(2)
                    take_xl1(3)
                if a:
                    stage_a(s + 1, after, 2)
                if b:
                    expo1(1)
                    low1(3)
                if a:
                    stage_a(s + 1, after, 3)
                if b:
                    take_head(s, 0)
                if c:
                    low(s, HEAD_2, logit2, lambda q: a2_low[:, q, :])
                if b:
                    expo1(2)
                if a:
                    stage_a(s + 1, after, 4)
                if b:
                    take_head(s, 1)
                    expo1(3)
                if c:
                    expo(s, HEAD_2, prob2, logit2)
                if b:
                    take_head(s, 2)
                    take_head(s, 3)
                if a:
                    stage_a(s + 1, after, 5)
                if b:
                    act.wait_ge(o_taken[1], o_turn.done(s, B_HEADS[3]))
                    nc.scalar.activation(logit[1][:], hid[:], ACT.Exp).then_inc(exp_h_ready, 1)
                if c:
                    if not (isinstance(s, int) and s == 1):
                        act.wait_ge(out_ready, nth(1, s - 2, 0))
                    for q in range(NB):
                        i = q % 2
                        act.wait_ge(rden2_ready, nth(2, s - 1, q // 2))
                        nc.scalar.activation(y2[:, q, :], bank_o[i][:, 0:F], ACT.Copy,
                                             scale=rden2[:, q:q + 1]).then_inc(o_taken[i], 1)

            schedule(act, stage_a, step, lambda g: None)

        @block.vector
        def _(dve):
            count = [0]

            def const(instruction):
                instruction.then_inc(vector_consts, 1)
                count[0] += 1
                dve.wait_ge(vector_consts, count[0])

            dve.wait_ge(bias3_in, 32)
            const(nc.vector.memset(bias_row[:, HD:HD + 2], 0.0))
            const(nc.vector.tensor_copy(bias_parts[:, 0, :], bias_row))
            const(nc.vector.tensor_tensor(bias_rest, bias_row, bias_parts[:, 0, :], ALU.subtract))
            const(nc.vector.tensor_copy(bias_parts[:, 1, :], bias_rest))
            const(nc.vector.tensor_tensor(bias_rest, bias_rest, bias_parts[:, 1, :], ALU.subtract))
            nc.vector.tensor_copy(bias_parts[:, 2, :], bias_rest).then_inc(bias_parts_ready, 1)
            dve.wait_ge(weights_in, WEIGHTS)
            dve.wait_ge(pool_consts, POOL_CONSTS)

            def through(w, vec, dst):
                const(nc.vector.tensor_tensor_reduce(scratch[:, 0:w.shape[-1]], w, vec, 1.0, 0.0, ALU.mult,
                                                     ALU.add, dst))
            for t in range(2):
                for k in range(KF):
                    through(w0_t[:, k, :], vec0[:, t, :], wa0[:, k, t:t + 1])
                    for h in range(H):
                        cols = slice(h * D, (h + 1) * D)
                        through(w1_t[:, k, cols], vec1[:, t, cols], wa1[:, k, t * H + h:t * H + h + 1])
                for k in range(KH):
                    through(w2_t[:, k, 2:], vec2[:, t, :], w2_t[:, k, t:t + 1])
            for k in range(KF):
                const(nc.vector.tensor_scalar(wa0_wide[:, k, :], ones[:], wa0[:, k, 0:1], None, ALU.mult))
            assert count[0] == VECTOR_CONSTS, count[0]

            sa = Steps(dve, a_steps, A_STEPS)
            st_b = Steps(dve, b_steps, B_STEPS)
            st_c = Steps(dve, c_steps, C_STEPS)
            st_n = Steps(dve, n_steps, N_STEPS)

            def gate(slot):
                nc.vector.memset(gate_t[:, slot:slot + 1], 0.0)

            def moments_of(st, slot, src, stats_t, moments_t, var_t, var_sem):
                for b in range(NB):
                    st.done(nc.vector.bn_stats(stats_t[:, b, :], src[:, b, :]))
                st.wait()
                gate(slot)
                for b in range(NB):
                    st.done(nc.vector.bn_aggr(moments_t[:, b, :], stats_t[:, b, :]))
                st.wait()
                nc.vector.tensor_scalar(var_t[:], moments_t[:, :, 1], EPS, None, ALU.add).then_inc(var_sem, 1)

            def normed(g, src, moments_t, rstd_t, rstd_sem, dst, ready):
                dve.wait_ge(rstd_sem, nth(1, g, 0))
                for b in range(NB):
                    last = nc.vector.tensor_scalar(dst[:, b, :], src[:, b, :], moments_t[:, b, 0:1],
                                                   rstd_t[:, b:b + 1], ALU.subtract, ALU.mult)
                last.then_inc(ready, 1)

            def stage_a(g, slot, piece):
                if piece == 0:
                    sa.begin(g)
                    dve.wait_ge(adj_in, nth(16, g, 15))
                    if not (isinstance(g, int) and g < 3):
                        dve.wait_ge(masked_ready, half_turn.done(g - 2, 2 * HEAD_2 + 1))
                    nc.vector.tensor_scalar(mask[slot][:], adj_t[:], 0.0, NO_EDGE, ALU.is_le,
                                            ALU.mult).then_inc(mask_ready, 1)
                if piece in (1, "mask_T"):
                    dve.wait_ge(a_full[1], nth(A_TURNS, g, A_MASK))
                    nc.vector.tensor_copy(mask_T[slot][:, 2:4, :], bank_a[1][:].bitcast(BF16)
                                          .rearrange("p (b n) -> p b n", b=2)).then_inc(a_taken[1], 1)
                if piece in (1, "s_j"):
                    dve.wait_ge(a_full[0], nth(A_TURNS, g, A_LOGIT))
                    sa.done(nc.vector.tensor_copy(sj[:, 0, :], bank_a[0][:, 0:NB]))
                    nc.vector.tensor_scalar(sj[:, 1, :], bank_a[0][:, 0:NB], SLOPE, None,
                                            ALU.mult).then_inc(a_taken[0], 1)
                if piece == 2:
                    sa.wait()
                    dve.wait_ge(low0_ready, nth(1, g, 0))
                    for b in range(NB):
                        last = nc.vector.scalar_tensor_tensor(out=logit0[:, b, :], in0=bank_a[1][:],
                                                              scalar=sj[:, 0, b:b + 1], in1=logit0[:, b, :],
                                                              op0=ALU.add, op1=ALU.max)
                    last.then_inc(a_taken[1], 1)
                    dve.wait_ge(a_taken[0], nth(A_TURNS, g, A_MASK))
                    dve.wait_ge(a_taken[1], nth(A_TURNS, g, A_LOGIT))
                    gate(5)
                    for b in range(NB):
                        sa.done(nc.vector.tensor_tensor_reduce(logit0[:, b, :], logit0[:, b, :],
                                                               mask_T[slot][:, b, :], 1.0, LOWEST, ALU.add,
                                                               ALU.max, top0[:, b:b + 1]))
                    sa.wait()
                    nc.vector.tensor_scalar(neg_top0[:], top0[:], -1.0, None,
                                            ALU.mult).then_inc(masked0_ready, 1)
                if piece == 3:
                    dve.wait_ge(prob0_ready, nth(1, g, 0))
                    nc.vector.reciprocal(rden0[:], den0[:]).then_inc(rden0_ready, 1)

                if piece == 4:
                    for i in range(2):
                        dve.wait_ge(a_taken[i], nth(A_TURNS, g, A_OUT))
                    nc.vector.scalar_tensor_tensor(out=leak0[:], in0=mix0[:], scalar=SLOPE, in1=mix0[:],
                                                   op0=ALU.mult, op1=ALU.max).then_inc(leak0_ready, 1)
                if piece == 5:
                    dve.wait_ge(a_full[1], nth(A_TURNS, g, A_X1T))
                    nc.vector.tensor_copy(x1T[:, 1, :], bank_a[1][:]).then_inc(a_taken[1], 1)
                if piece == 6:
                    st_b.begin(g)
                    cols1(g)
                if piece == 7:
                    small_rows(g, AROW1, a_rows, 3 * H)

            def moments_a(g):
                dve.wait_ge(sum0_ready, nth(1, g, 0))
                moments_of(sa, 6, leak0, stats, moments, var_eps, var_ready)

            def normed_a(g, slot):
                normed(g, leak0, moments, rstd, rstd_ready, x1[slot], x1_ready)
                sa.end()

            def split(st, src, r, parts, n):
                st.done(nc.vector.tensor_copy(parts[:, :, 0:n], src))
                st.wait()
                st.done(nc.vector.tensor_tensor(r, src, parts[:, :, 0:n], ALU.subtract))
                st.wait()
                st.done(nc.vector.tensor_copy(parts[:, :, n:2 * n], r))
                st.wait()
                st.done(nc.vector.tensor_tensor(r, r, parts[:, :, n:2 * n], ALU.subtract))
                st.wait()
                nc.vector.tensor_copy(parts[:, :, 2 * n:3 * n], r).then_inc(parts_ready, 1)

            def maxima(s, m, slot_g, top_of, bank_at):
                i, turn = bank_at
                dve.wait_ge(row_full[i], row_turn[i].done(s, turn))
                gate(slot_g)
                for b in range(NB):
                    last = nc.vector.tensor_tensor_reduce(junk[:, i, b, :], bank_row[i][:], m[:, b, :], 1.0,
                                                          LOWEST, ALU.add, ALU.max, top_of(b))
                last.then_inc(row_taken[i], 1)

            def shifts(st, b_cols, n, t, c, vv, r, parts):
                st.done(nc.vector.tensor_tensor(t, t, b_cols, ALU.add))
                st.wait()
                st.done(nc.vector.scalar_tensor_tensor(out=c, in0=t, scalar=SLOPE, in1=t, op0=ALU.mult,
                                                       op1=ALU.max))
                st.wait()
                st.done(nc.vector.tensor_tensor(vv[:, :, 0:n], b_cols, c, ALU.subtract))
                st.done(nc.vector.scalar_tensor_tensor(out=vv[:, :, n:2 * n], in0=b_cols, scalar=SLOPE,
                                                       in1=c, op0=ALU.mult, op1=ALU.subtract))
                st.wait()
                split(st, vv[:], r, parts, 2 * n)

            def joined(s, n, t, bank_at, a_of):
                i, turn = bank_at
                dve.wait_ge(row_full[i], row_turn[i].done(s, turn))
                dve.wait_ge(low_ready, head_turn.done(s, n))
                for b in range(NB):
                    last = nc.vector.scalar_tensor_tensor(out=t[:, b, :], in0=bank_row[i][:], scalar=a_of(b),
                                                          in1=t[:, b, :], op0=ALU.add, op1=ALU.max)
                last.then_inc(row_taken[i], 1)

            def denominators(s, n):
                for i in range(2):
                    dve.wait_ge(o_full[i], o_turn.done(s, B_HEADS[n]))
                    if n:
                        dve.wait_ge(o_taken[i], o_turn.done(s, B_HEADS[n - 1]))
                    den = bank_o[i][:, 0:2 * (D + 1)].rearrange("p (b f) -> p b f", b=2)[:, :, D]
                    nc.vector.reciprocal(rden[:, 2 * i:2 * i + 2], den).then_inc(rden_ready, 1)

            def small_rows(s, turn, dst, n):
                dve.wait_ge(small_full, small_turn.done(s, turn))
                nc.vector.tensor_copy(dst[:], bank_small[0:n, 0:N // 2].bitcast(BF16)).then_inc(small_taken, 1)

            def cols1(s):
                dve.wait_ge(small_full, small_turn.done(s, COLS1))
                nc.vector.tensor_copy(ab[:], bank_small[:, 0:NB * 2 * H]
                                      .rearrange("p (b c) -> p b c", b=NB)).then_inc(small_taken, 1)
                dve.wait_ge(small_taken, small_turn.done(s, COLS1))
                nc.vector.tensor_scalar(a_low[:], ab[:, :, 0:H], SLOPE, None, ALU.mult).then_inc(a_low_ready, 1)
                split(st_b, ab[:, :, 0:H], rest[:, :, 0:H], a_parts, H)

            def cols2(s):
                for i in range(2):
                    dve.wait_ge(o_taken[i], o_turn.done(s, C_XL + 1))
                nc.vector.tensor_scalar(a2_low[:], xl2[:, :, 0:1], SLOPE, None, ALU.mult).then_inc(a_low_ready, 1)
                split(st_c, xl2[:, :, 0:1], rest2[:, :, 0:1], a2_parts, 1)

            def tail_moments(g):
                st_n.begin(g)
                dve.wait_ge(sum2_ready, nth(1, g, 0))
                moments_of(st_n, 7, y2, stats2, moments2, var_eps2, var2_ready)
                st_n.end()

            def tail_normed(g):
                if not (isinstance(g, int) and g == 0):
                    dve.wait_ge(out_stored, nth(16, g - 1, 15))
                normed(g, y2, moments2, rstd2, rstd2_ready, out_t, out_ready)

            def step(s, slot, a, b, c):
                before, after = (slot + 2) % 3, (slot + 1) % 3

                def maxima1(n):
                    maxima(s, mask_T[slot], n, lambda q: top[:, q, n:n + 1], ROW_A1[n])

                def joined1(n):
                    joined(s, HEAD_1[n], logit[n % 2], ROW_V1[n], lambda q: ab[:, q, n:n + 1])

                def denominators2(half):
                    for i in range(2):
                        q = 2 * half + i
                        dve.wait_ge(o_full[i], o_turn.done(s, C_OUT[half]))
                        last = nc.vector.reciprocal(rden2[:, q:q + 1], bank_o[i][:, F:F + 1])
                    last.then_inc(rden2_ready, 1)

                if b:
                    dve.wait_ge(self_edges, nth(1, s, 0))
                    maxima1(0)
                if a:
                    stage_a(s + 1, after, 0)
                if b:
                    maxima1(1)
                    maxima1(2)
                    maxima1(3)
                    for i in range(2):
                        dve.wait_ge(row_taken[i], row_turn[i].done(s, 1))
                    st_b.resume(s)
                    shifts(st_b, ab[:, :, H:2 * H], H, top[:], shift[:], v, rest[:], v_parts)
                    st_b.end()
                if a:
                    stage_a(s + 1, after, "mask_T")
                if c:
                    st_c.begin(s - 1)
                    cols2(s)
                if b:
                    small_rows(s, VROW1, v_rows, 6 * H)
                if c:
                    small_rows(s, AROW2, a2_rows, 3)
                if c:
                    maxima(s, mask_T[before], 4, lambda q: top2[:, q, :], ROW_A2)
                    dve.wait_ge(row_taken[0], row_turn[0].done(s, ROW_A2[1]))
                    shifts(st_c, xl2[:, :, 1:2], 1, top2[:], shift2[:], v_2, rest2[:], v2_parts)
                    st_c.end()
                if b:
                    joined1(0)
                if c:
                    small_rows(s, VROW2, v2_rows, 6)
                if a:
                    stage_a(s + 1, after, "s_j")
                if b:
                    joined1(1)
                if a:
                    stage_a(s + 1, after, 2)
                if b:
                    joined1(2)
                if a:
                    stage_a(s + 1, after, 3)
                if b:
                    joined1(3)
                    denominators(s, 0)
                if c and tail_of(s):
                    tail_moments(s - 2)
                if c:
                    joined(s, HEAD_2, logit2, ROW_V2, lambda q: xl2[:, q, 0:1])
                if a:
                    stage_a(s + 1, after, 4)
                if b:
                    denominators(s, 1)
                if c and tail_of(s):
                    tail_normed(s - 2)
                if a:
                    moments_a(s + 1)
                if b:
                    denominators(s, 2)
                if a:
                    normed_a(s + 1, after)
                if b:
                    denominators(s, 3)
                if a:
                    stage_a(s + 1, after, 5)
                if b:
                    for i in range(2):
                        dve.wait_ge(o_taken[i], o_turn.done(s, B_HEADS[3]))
                    nc.vector.tensor_scalar(logit[0][:], hid[:], 0.0, -1.0, ALU.max,
                                            ALU.add).then_inc(elu_high_ready, 1)
                if c:
                    denominators2(0)
                if b:
                    dve.wait_ge(exp_h_ready, nth(1, s, 0))
                    dve.wait_ge(elu_high_ready, nth(1, s, 0))
                    nc.vector.scalar_tensor_tensor(out=hid[:], in0=logit[1][:], scalar=1.0, in1=logit[0][:],
                                                   op0=ALU.min, op1=ALU.add).then_inc(hid_ready, 1)
                if a:
                    stage_a(s + 1, after, 6)
                if c:
                    denominators2(1)
                if a:
                    stage_a(s + 1, after, 7)

            def finish(g):
                tail_moments(g)
                tail_normed(g)

            def stage_a_whole(g, slot, piece):
                stage_a(g, slot, piece)
                if piece == 4:
                    moments_a(g)
                    normed_a(g, slot)

            schedule(dve, stage_a_whole, step, finish)

        @block.tensor
        def _(pe):
            pe.wait_ge(pool_consts, POOL_CONSTS)
            pe.wait_ge(vector_consts, VECTOR_CONSTS)
            pe.wait_ge(weights_in, WEIGHTS)
            pe.wait_ge(bias3_in, 3 * 16)

            def a_free(i, g, turn):
                if turn or not (isinstance(g, int) and g == 0):
                    pe.wait_ge(a_taken[i], g * A_TURNS + turn)

            def free(semaphore, turns, s, turn):
                n = turns.before(s, turn)
                if not (isinstance(n, int) and n == 0):
                    pe.wait_ge(semaphore, n)

            def stage_a(g, slot, piece):
                if piece == 0:
                    pe.wait_ge(x_in, nth(16, g, 15))
                    for k in range(KF):
                        a_free(k, g, A_X)
                        for b in range(NB):
                            last = nc.tensor.transpose(bank_a[k][:, b * P:(b + 1) * P],
                                                       x_t[:, b, k * P:(k + 1) * P], ident[:])
                        last.then_inc(a_full[k], 1)
                    pe.wait_ge(mask_ready, nth(1, g, 0))
                    for i in range(2):
                        a_free(i, g, A_MASK)
                        rows = bank_a[i][:].bitcast(BF16).rearrange("p (b n) -> p b n", b=2)
                        for j in range(2):
                            for b in range(NB):
                                d = 2 * i + j
                                last = nc.tensor.transpose(rows[:, j, b * P:(b + 1) * P],
                                                           mask[slot][:, b, d * P:(d + 1) * P], ident_b[:])
                        last.then_inc(a_full[i], 1)
                if piece in (1, "s_j"):
                    for i in range(2):
                        pe.wait_ge(a_taken[i], nth(A_TURNS, g, A_X))
                    a_free(0, g, A_LOGIT)
                    for b in range(NB):
                        for k in range(KF):
                            last = nc.tensor.matmul(bank_a[0][:, b:b + 1], xT[:, k, b * P:(b + 1) * P],
                                                    wa0[:, k, 1:2], start=(k == 0), stop=(k == KF - 1))
                    last.then_inc(a_full[0], 1)
                if piece in (1, "s_i"):
                    a_free(1, g, A_LOGIT)
                    for k in range(KF):
                        last = nc.tensor.matmul(bank_a[1][:], wa0_wide[:, k, :], xT[:, k, :],
                                                start=(k == 0), stop=(k == KF - 1))
                    last.then_inc(a_full[1], 1)
                if piece == 2:
                    for i in range(2):
                        a_free(i, g, A_VALUES)
                    for b in range(NB):
                        for k in range(KF):
                            last = nc.tensor.matmul(bank_a[b // 2][:, (b % 2) * F:(b % 2 + 1) * F],
                                                    xT[:, k, b * P:(b + 1) * P], w0_t[:, k, :],
                                                    start=(k == 0), stop=(k == KF - 1))
                        if b % 2:
                            last.then_inc(a_full[b // 2], 1)
                if piece == 3:
                    pe.wait_ge(prob0_ready, nth(1, g, 0))
                    for i in range(2):
                        a_free(i, g, A_OUT)
                    for b in range(NB):
                        for k in range(NB):
                            last = nc.tensor.matmul(bank_a[b // 2][:, (b % 2) * F:(b % 2 + 1) * F],
                                                    prob0[:, k, b * P:(b + 1) * P], values0[:, k, :],
                                                    start=(k == 0), stop=(k == NB - 1))
                        if b % 2:
                            last.then_inc(a_full[b // 2], 1)
                if piece == 5:
                    pe.wait_ge(x1_ready, nth(1, g, 0))
                    for k in range(KF):
                        a_free(k, g, A_X1T)
                        for b in range(NB):
                            last = nc.tensor.transpose(bank_a[k][:, b * P:(b + 1) * P],
                                                       x1[slot][:, b, k * P:(k + 1) * P], ident[:])
                        last.then_inc(a_full[k], 1)
                if piece == 6:
                    for k in range(KF):
                        pe.wait_ge(a_taken[k], nth(A_TURNS, g, A_X1T))
                    free(small_taken, small_turn, g, COLS1)
                    for q in range(NB):
                        for k in range(KF):
                            last = nc.tensor.matmul(bank_small[:, q * 2 * H:(q + 1) * 2 * H],
                                                    x1T[:, k, q * P:(q + 1) * P], wa1[:, k, :],
                                                    start=(k == 0), stop=(k == KF - 1))
                    last.then_inc(small_full, 1)
                if piece == 7:
                    small(g, AROW1, PARTS_A1, a_parts, 3 * H)
                    pe.wait_ge(small_taken, small_turn.done(g, AROW1))
                    row(g, ROW_A1[0], pick_a1, 0, a_rows)
                    row(g, ROW_A1[1], pick_a1, 1, a_rows)

            def small(s, turn, ready, parts, n):
                pe.wait_ge(parts_ready, parts_turn.done(s, ready))
                free(small_taken, small_turn, s, turn)
                rows = bank_small[0:n, 0:N // 2].bitcast(BF16)
                for b in range(NB):
                    last = nc.tensor.transpose(rows[:, b * P:(b + 1) * P], parts[:, b, :], ident_b[:])
                last.then_inc(small_full, 1)

            def row(s, bank_at, pick, q, rows):
                i, turn = bank_at
                free(row_taken[i], row_turn[i], s, turn)
                nc.tensor.matmul(bank_row[i][:], pick[:, q, :], rows[:], start=True,
                                 stop=True).then_inc(row_full[i], 1)

            def logit_rows(s, n, bank_at, pick, q, rows):
                row(s, bank_at, pick, q, rows)
                free(low_ready, head_turn, s, n)
                nc.tensor.matmul(bank_v2[:], pick[:, q + pick.shape[1] // 2, :], rows[:], start=True,
                                 stop=True).then_inc(v2_full, 1)

            def step(s, slot, a, b, c):
                after = (slot + 1) % 3

                def xl2_block(q):
                    i = q % 2
                    for j in range(2):
                        if q == 0 or j == i:
                            free(o_taken[j], o_turn, s, C_XL + q // 2)
                    nc.tensor.matmul(bank_o[i][:, 0:2 + F], ones3[:], bias3[:, HD:], start=True, stop=False)
                    for k in range(KH):
                        last = nc.tensor.matmul(bank_o[i][:, 0:2 + F], hid_T[:, k, q * P:(q + 1) * P],
                                                w2_t[:, k, :], start=False, stop=(k == KH - 1))
                    last.then_inc(o_full[i], 1)

                def xl1_block(q):
                    free(o_taken[q % 2], o_turn, s, B_XL + q // 2)
                    nc.tensor.matmul(bank_o[q % 2][:], ones3[:], bias3[:, 0:HD], start=True, stop=False)
                    for k in range(KF):
                        last = nc.tensor.matmul(bank_o[q % 2][:], x1T[:, k, q * P:(q + 1) * P], w1_t[:, k, :],
                                                start=False, stop=(k == KF - 1))
                    last.then_inc(o_full[q % 2], 1)

                def product2(half):
                    if half == 0:
                        pe.wait_ge(prob_ready, head_turn.done(s, HEAD_2))
                    for i in range(2):
                        q = 2 * half + i
                        free(o_taken[i], o_turn, s, C_OUT[half])
                        for k in range(NB):
                            last = nc.tensor.matmul(bank_o[i][:, 0:F + 1], prob2[:, k, q * P:(q + 1) * P],
                                                    xl2[:, k, 2:], start=(k == 0), stop=(k == NB - 1))
                        last.then_inc(o_full[i], 1)

                def rows1(n):
                    logit_rows(s, HEAD_1[n], ROW_V1[n], pick_v1, n, v_rows)

                def head(n):
                    if n == 0:
                        for i in range(2):
                            pe.wait_ge(o_taken[i], o_turn.done(s, B_XL + 1))
                    pe.wait_ge(prob_ready, head_turn.done(s, HEAD_1[n]))
                    for q in range(NB):
                        i = q // 2
                        if q % 2 == 0:
                            free(o_taken[i], o_turn, s, B_HEADS[n])
                        for k in range(NB):
                            last = nc.tensor.matmul(bank_o[i][:, (q % 2) * (D + 1):(q % 2 + 1) * (D + 1)],
                                                    prob[n % 2][:, k, q * P:(q + 1) * P], xl1[:, k, n, :],
                                                    start=(k == 0), stop=(k == NB - 1))
                        if q % 2:
                            last.then_inc(o_full[i], 1)

                if c:
                    pe.wait_ge(hid_ready, nth(1, s - 1, 0))
                    for k in range(KH):
                        free(o_taken[k % 2], o_turn, s, C_HT + k // 2)
                        for q in range(NB):
                            last = nc.tensor.transpose(bank_o[k % 2][:, q * P:(q + 1) * P],
                                                       hid[:, q, k * P:(k + 1) * P], ident[:])
                        last.then_inc(o_full[k % 2], 1)
                if b:
                    row(s, ROW_A1[2], pick_a1, 2, a_rows)
                if c:
                    xl2_block(0)
                    xl2_block(1)
                if b:
                    row(s, ROW_A1[3], pick_a1, 3, a_rows)
                if c:
                    xl2_block(2)
                    xl2_block(3)
                if a:
                    stage_a(s + 1, after, 0)
                if b:
                    small(s, VROW1, PARTS_V1, v_parts, 6 * H)
                if c:
                    small(s, AROW2, PARTS_A2, a2_parts, 3)
                if b:
                    pe.wait_ge(small_taken, small_turn.done(s, VROW1))
                    rows1(0)
                if c:
                    pe.wait_ge(small_taken, small_turn.done(s, AROW2))
                    row(s, ROW_A2, pick_a2, 0, a2_rows)
                if b:
                    rows1(1)
                if c:
                    small(s, VROW2, PARTS_V2, v2_parts, 6)
                if a:
                    stage_a(s + 1, after, 1)
                if b:
                    xl1_block(0)
                    xl1_block(1)
                    rows1(2)
                    xl1_block(2)
                    xl1_block(3)
                    head(0)
                    rows1(3)
                if a:
                    stage_a(s + 1, after, 2)
                if c:
                    pe.wait_ge(small_taken, small_turn.done(s, VROW2))
                    logit_rows(s, HEAD_2, ROW_V2, pick_v2, 0, v2_rows)
                if a:
                    stage_a(s + 1, after, 3)
                if b:
                    head(1)
                    head(2)
                    head(3)
                if a:
                    stage_a(s + 1, after, 5)
                if c:
                    product2(0)
                if a:
                    stage_a(s + 1, after, 6)
                if c:
                    product2(1)
                if a:
                    stage_a(s + 1, after, 7)

            schedule(pe, stage_a, step, lambda g: None)


_INS = ['x', 'adj', 'L0_gnn_W', 'L0_gnn_a', 'L1_gnn_W1', 'L1_gnn_att_src1', 'L1_gnn_att_dst1', 'L1_gnn_b1',
        'L1_gnn_W2', 'L1_gnn_att_src2', 'L1_gnn_att_dst2', 'L1_gnn_b2']


def kernel(**inputs):
    import numpy as _np
    import concourse.bacc as _bacc
    from concourse.bass_utils import run_bass_kernel_spmd as _run

    nc = _bacc.Bacc("TRN2", target_bir_lowering=False, num_devices=1)
    arrays, args = {}, []
    for name in _INS:
        a = _np.ascontiguousarray(inputs[name])
        arrays[f"in_{name}_dram"] = a
        args.append(nc.dram_tensor(f"in_{name}_dram", a.shape, mybir.dt.from_np(a.dtype), kind="ExternalInput").ap())
    args.append(nc.dram_tensor("out_0_dram", inputs['x'].shape, F32, kind="ExternalOutput").ap())
    build(nc, *args)
    r = _run(nc, [arrays], core_ids=[0])
    return r.results[0]["out_0_dram"]
```

```python
from contextlib import ExitStack

import concourse.bass as bass
from concourse import mybir

F32 = mybir.dt.float32
BF16 = mybir.dt.bfloat16
I32 = mybir.dt.int32
ALU = mybir.AluOpType
ACT = mybir.ActivationFunctionType

P = 128
SLOPE = 0.2
EPS = 1e-5
NO_EDGE = -9.0e15
LOWEST = -3.0e38

A_X, A_MASK, A_LOGIT, A_VALUES, A_OUT, A_X1T, A_TURNS = range(7)
C_HT, C_XL, C_OUT = (0, 1), (2, 3), (10, 11)
B_XL, B_HEADS = (4, 5), (6, 7, 8, 9)
COLS1, AROW1, VROW1, AROW2, VROW2 = range(5)
PARTS_A1, PARTS_V1, PARTS_A2, PARTS_V2 = range(4)
HEAD_1, HEAD_2 = (0, 1, 2, 3), 4
ROW_A1 = [(0, 0), (1, 0), (0, 1), (1, 1)]
ROW_V1 = [(0, 2), (1, 2), (1, 3), (0, 4)]
ROW_A2, ROW_V2 = (0, 3), (1, 4)
PIECES_A = ("make mask", "x", "mask", "s_j", "s_i", "low", "joined", "exp", "1 / den", "values", "scale",
            "attention", "mix 0", "mix 1", "self edges", "leaky", "sum", "norm", "x1T", "cols", "rows",
            "row 0", "row 1", "row 2", "row 3")
A_STEPS, B_STEPS, C_STEPS, N_STEPS = 13, 12, 12, 8


def nth(per_graph, g, k):
    return g * per_graph + (k + 1)


class Turns:

    def __init__(self, owners, steps):
        self.owners, self.steps = owners, steps

    def before(self, step, k):
        n = step * len(self.owners) + k
        if isinstance(step, int) and step == 0:
            return n - self.owners[:k].count("C")
        if isinstance(step, int) and step == self.steps:
            n = n - self.owners[:k].count("B")
        return n - self.owners.count("C")

    def done(self, step, k):
        return self.before(step, k) + 1


class Steps:

    def __init__(self, engine, semaphore, per_graph):
        self.engine, self.semaphore, self.per_graph = engine, semaphore, per_graph

    def begin(self, g):
        self.g, self.k = g, 0

    def resume(self, g):
        self.g = g

    def done(self, instruction):
        instruction.then_inc(self.semaphore, 1)
        self.k += 1

    def wait(self):
        self.engine.wait_ge(self.semaphore, nth(self.per_graph, self.g, self.k - 1))

    def end(self):
        assert self.k == self.per_graph, (self.semaphore, self.k)


def build(nc, x, adj, w0, a0, w1, src1, dst1, b1, w2, src2, dst2, b2, out):
    G, N, F = x.shape
    NB = N // P
    KF = F // P
    H = src1.shape[0]
    D = src1.shape[1]
    HD = H * D
    KH = HD // P
    assert N == 512 and D == P and F == 256 and H == 4 and G % 2 == 0

    with ExitStack() as ctx:
        def sb(name, shape, dt=F32):
            return ctx.enter_context(nc.sbuf_tensor(name, shape, dt))

        def bank(name):
            return ctx.enter_context(nc.psum_tensor(name, [P, 512], F32))

        def sem(name):
            return ctx.enter_context(nc.semaphore(name))

        ident = sb("ident", [P, P])
        ident_b = sb("ident_b", [P, P], BF16)
        off_diag = sb("off_diag", [P, P], BF16)
        ones = sb("ones", [P, P])
        pick_a1 = sb("pick_a1", [3 * H, H, P], BF16)
        pick_v1 = sb("pick_v1", [6 * H, 2 * H, P], BF16)
        pick_a2 = sb("pick_a2", [3, 1, P], BF16)
        pick_v2 = sb("pick_v2", [6, 2, P], BF16)
        w0_t = sb("w0_t", [P, KF, F])
        w1_t = sb("w1_t", [P, KF, HD])
        w2_t = sb("w2_t", [P, KH, 2 + F])
        wa0 = sb("wa0", [P, KF, 2])
        wa1 = sb("wa1", [P, KF, 2 * H])
        wa0_wide = sb("wa0_wide", [P, KF, P])
        bias_parts = sb("bias_parts", [1, 3, HD + 2 + F], BF16)
        bias3 = sb("bias3", [3, HD + 2 + F], BF16)
        ones3 = sb("ones3", [3, P], BF16)
        minus_half = sb("minus_half", [P, NB])
        gate_t = sb("gate_t", [P, 9])

        x_t = sb("x_t", [P, NB, F])
        adj_t = sb("adj_t", [P, NB, N], I32)
        mask = [sb(f"mask{i}", [P, NB, N], BF16) for i in range(3)]
        mask_T = [sb(f"mask_T{i}", [P, NB, N], BF16) for i in range(3)]
        x1 = [sb(f"x1_{i}", [P, NB, F]) for i in range(3)]
        xT = sb("xT", [P, KF, N])
        sj = sb("sj", [P, 2, NB])
        logit0 = sb("logit0", [P, NB, N])
        prob0 = sb("prob0", [P, NB, N])
        top0 = sb("top0", [P, NB])
        neg_top0 = sb("neg_top0", [P, NB])
        den0 = sb("den0", [P, NB])
        rden0 = sb("rden0", [P, NB])
        values0 = sb("values0", [P, NB, F])
        mix0 = sb("mix0", [P, NB, F])
        leak0 = sb("leak0", [P, NB, F])
        stats = sb("stats", [P, NB, 6])
        moments = sb("moments", [P, NB, 2])
        var_eps = sb("var_eps", [P, NB])
        rstd = sb("rstd", [P, NB])
        x1T = sb("x1T", [P, KF, N])
        ab = sb("ab", [P, NB, 2 * H])
        a_low = sb("a_low", [P, NB, H])
        a2_low = sb("a2_low", [P, NB, 1])
        rest = sb("rest", [P, NB, 2 * H])
        a_parts = sb("a_parts", [P, NB, 3 * H], BF16)
        v_parts = sb("v_parts", [P, NB, 6 * H], BF16)
        a2_parts = sb("a2_parts", [P, NB, 3], BF16)
        v2_parts = sb("v2_parts", [P, NB, 6], BF16)
        a_rows = sb("a_rows", [3 * H, N], BF16)
        v_rows = sb("v_rows", [6 * H, N], BF16)
        a2_rows = sb("a2_rows", [3, N], BF16)
        v2_rows = sb("v2_rows", [6, N], BF16)
        top = sb("top", [P, NB, H])
        shift = sb("shift", [P, NB, H])
        v = sb("v", [P, NB, 2 * H])
        rest2 = sb("rest2", [P, NB, 2])
        top2 = sb("top2", [P, NB, 1])
        shift2 = sb("shift2", [P, NB, 1])
        v_2 = sb("v_2", [P, NB, 2])
        rden2 = sb("rden2", [P, NB])
        junk = sb("junk", [P, 2, NB, N], BF16)
        logit2 = sb("logit2", [P, NB, N])
        prob2 = sb("prob2", [P, NB, N])
        xl1 = sb("xl1", [P, NB, H, D + 1])
        xl2 = sb("xl2", [P, NB, 2 + F + 1])
        logit = [sb(f"logit1_{i}", [P, NB, N]) for i in range(2)]
        prob = [sb(f"prob1_{i}", [P, NB, N]) for i in range(2)]
        rden = sb("rden", [P, NB])
        hid = sb("hid", [P, NB, HD])
        hid_line = hid[0:1, :, :].rearrange("p b n -> p (b n)")
        bias_row = hid_line[:, 0:HD + 2 + F]
        bias_rest = hid_line[:, HD + 2 + F:2 * (HD + 2 + F)]
        hid_T = sb("hid_T", [P, KH, N])
        vec1 = hid_T[:, 0:2, :]
        vec0 = hid_T[:, 2, :].rearrange("p (t f) -> p t f", t=2)
        vec2 = hid_T[:, 3, :].rearrange("p (t f) -> p t f", t=2)
        y2 = sb("y2", [P, NB, F])
        stats2 = sb("stats2", [P, NB, 6])
        moments2 = sb("moments2", [P, NB, 2])
        var_eps2 = sb("var_eps2", [P, NB])
        rstd2 = sb("rstd2", [P, NB])
        out_t = sb("out_t", [P, NB, F])

        bank_a = [bank(f"bank_a{i}") for i in range(2)]
        bank_small = bank("bank_small")
        bank_row = [bank(f"bank_row{i}") for i in range(2)]
        bank_v2 = bank("bank_v2")
        bank_o = [bank(f"bank_o{i}") for i in range(2)]

        a_full = [sem(f"a_full{i}") for i in range(2)]
        a_taken = [sem(f"a_taken{i}") for i in range(2)]
        small_full, small_taken = sem("small_full"), sem("small_taken")
        row_full = [sem(f"row_full{i}") for i in range(2)]
        row_taken = [sem(f"row_taken{i}") for i in range(2)]
        v2_full = sem("v2_full")
        o_full = [sem(f"o_full{i}") for i in range(2)]
        o_taken = [sem(f"o_taken{i}") for i in range(2)]

        weights_in = sem("weights_in")
        bias_parts_ready = sem("bias_parts_ready")
        bias3_in = sem("bias3_in")
        pool_consts = sem("pool_consts")
        vector_consts = sem("vector_consts")
        x_in = sem("x_in")
        adj_in = sem("adj_in")
        out_stored = sem("out_stored")
        mask_ready = sem("mask_ready")
        self_edges = sem("self_edges")
        low0_ready = sem("low0_ready")
        masked0_ready = sem("masked0_ready")
        prob0_ready = sem("prob0_ready")
        rden0_ready = sem("rden0_ready")
        leak0_ready = sem("leak0_ready")
        sum0_ready = sem("sum0_ready")
        var_ready = sem("var_ready")
        rstd_ready = sem("rstd_ready")
        x1_ready = sem("x1_ready")
        a_steps = sem("a_steps")
        b_steps = sem("b_steps")
        n_steps = sem("n_steps")
        c_steps = sem("c_steps")
        parts_ready = sem("parts_ready")
        a_low_ready = sem("a_low_ready")
        low_half_ready = sem("low_half_ready")
        joined_half_ready = sem("joined_half_ready")
        low_ready = sem("low_ready")
        masked_ready = sem("masked_ready")
        prob_ready = sem("prob_ready")
        rden_ready = sem("rden_ready")
        exp_h_ready = sem("exp_h_ready")
        elu_high_ready = sem("elu_high_ready")
        hid_ready = sem("hid_ready")
        rden2_ready = sem("rden2_ready")
        sum2_ready = sem("sum2_ready")
        var2_ready = sem("var2_ready")
        rstd2_ready = sem("rstd2_ready")
        out_ready = sem("out_ready")

        POOL_CONSTS, VECTOR_CONSTS = 26, 5 + 2 * (KF * (1 + H) + KH) + KF
        WEIGHTS = 8 * 16

        block = ctx.enter_context(nc.Block())

        o_turn = Turns("CCCCBBBBBBCC", G)
        small_turn = Turns("BBBCC", G)
        row_turn = [Turns("BBBCB", G), Turns("BBBBC", G)]
        head_turn = Turns("BBBBC", G)
        half_turn = Turns("BBBBBBBBCC", G)
        parts_turn = Turns("BBCC", G)
        layer_turn = Turns("BC", G)

        def schedule(engine, stage_a, step, finish):
            for piece in PIECES_A:
                stage_a(0, 0, piece)
            step(0, 0, True, True, False)
            step(1, 1, True, True, True)
            step(2, 2, True, True, True)
            assert (G - 4) % 3 == 0
            with engine.Fori(3, G - 1, 3) as i:
                for r in range(3):
                    step(i + r, r, True, True, True)
            step(G - 1, (G - 1) % 3, False, True, True)
            step(G, G % 3, False, False, True)
            finish(G - 1)

        def tail_of(step):
            return not (isinstance(step, int) and step < 2)

        @block.sync
        def _(sp):
            for tile, src in (
                (w0_t[:], w0.rearrange("(k p) n -> p k n", p=P)),
                (w1_t[:], w1.rearrange("(k p) n -> p k n", p=P)),
                (w2_t[:, :, 2:], w2.rearrange("(k p) n -> p k n", p=P)),
                (vec0, a0.rearrange("(a t f) o -> a t (f o)", a=1, t=2).broadcast_to([P, 2, F])),
                (vec1[:, 0, :], src1.rearrange("(a h) f -> a (h f)", a=1).broadcast_to([P, HD])),
                (vec1[:, 1, :], dst1.rearrange("(a h) f -> a (h f)", a=1).broadcast_to([P, HD])),
                (vec2[:, 0, :], src2.broadcast_to([P, F])),
                (vec2[:, 1, :], dst2.broadcast_to([P, F])),
            ):
                sp.dma_start(tile, src).then_inc(weights_in, 16)
            sp.dma_start(bias_row[:, 0:HD], b1.rearrange("(a f) -> a f", a=1)).then_inc(bias3_in, 16)
            sp.dma_start(bias_row[:, HD + 2:], b2.rearrange("(a f) -> a f", a=1)).then_inc(bias3_in, 16)

            def load(g, reused=True):
                if reused:
                    sp.wait_ge(mask_ready, nth(1, g - 1, 0))
                sp.dma_start(adj_t[:], adj[g].rearrange("(b p) n -> p b n", p=P)).then_inc(adj_in, 16)
                if reused:
                    sp.wait_ge(sum0_ready, nth(1, g - 1, 0))
                sp.dma_start(x_t[:], x[g].rearrange("(b p) n -> p b n", p=P)).then_inc(x_in, 16)

            def store(g):
                sp.wait_ge(out_ready, nth(1, g, 0))
                sp.dma_start(out[g].rearrange("(b p) n -> p b n", p=P), out_t[:]).then_inc(out_stored, 16)

            load(0, False)
            sp.wait_ge(bias_parts_ready, 1)
            sp.dma_start(bias3[:], bias_parts[:]).then_inc(bias3_in, 16)
            load(1)
            load(2)
            load(3)
            with sp.Fori(4, G, 1) as i:
                store(i - 4)
                load(i)
            store(G - 4)
            store(G - 3)
            store(G - 2)
            store(G - 1)
            sp.wait_ge(out_stored, 16 * G)

        @block.gpsimd
        def _(pool):
            count = [0]

            def const(instruction):
                instruction.then_inc(pool_consts, 1)
                count[0] += 1
                pool.wait_ge(pool_consts, count[0])

            const(nc.gpsimd.memset(ones[:], 1.0))
            const(nc.gpsimd.memset(ones3[:], 1.0))
            const(nc.gpsimd.memset(minus_half[:], -0.5))
            const(nc.gpsimd.memset(xl1[:, :, :, D:D + 1], 1.0))
            const(nc.gpsimd.memset(xl2[:, :, 2 + F:], 1.0))
            const(nc.gpsimd.memset(ident[:], 0.0))
            const(nc.gpsimd.affine_select(out=ident[:], in_=ident[:], compare_op=ALU.not_equal, fill=1.0,
                                          base=0, pattern=[[-1, P]], channel_multiplier=1))
            const(nc.gpsimd.tensor_copy(ident_b[:], ident[:]))
            const(nc.gpsimd.memset(off_diag[:], 1.0))
            const(nc.gpsimd.affine_select(out=off_diag[:], in_=off_diag[:], compare_op=ALU.not_equal,
                                          fill=0.0, base=0, pattern=[[-1, P]], channel_multiplier=1))
            for pick, q in ((pick_a1, H), (pick_v1, 2 * H), (pick_a2, 1), (pick_v2, 2)):
                const(nc.gpsimd.memset(pick[:], 0.0))
                for part in range(3):
                    const(nc.gpsimd.affine_select(out=pick[:], in_=pick[:], compare_op=ALU.not_equal,
                                                  fill=1.0, base=-part * q, pattern=[[-1, q], [0, P]],
                                                  channel_multiplier=1))
            assert count[0] == POOL_CONSTS
            pool.wait_ge(vector_consts, VECTOR_CONSTS)

            def norm(g, var_sem, var, rstd_t, rstd_sem):
                pool.wait_ge(var_sem, nth(1, g, 0))
                nc.gpsimd.tensor_tensor(rstd_t[:], var[:], minus_half[:], ALU.pow).then_inc(rstd_sem, 1)

            def stage_a(g, slot, piece):
                if piece == "self edges":
                    pool.wait_ge(masked0_ready, nth(1, g, 0))
                    for m in (mask_T[slot], mask[slot]):
                        for b in range(NB):
                            d = m[:, b, b * P:(b + 1) * P]
                            last = nc.gpsimd.tensor_tensor(d, d, off_diag[:], ALU.mult)
                    last.then_inc(self_edges, 1)
                if piece == "sum":
                    pool.wait_ge(leak0_ready, nth(1, g, 0))
                    nc.gpsimd.tensor_tensor(leak0[:], leak0[:], x_t[:], ALU.add).then_inc(sum0_ready, 1)
                if piece == "norm":
                    norm(g, var_ready, var_eps, rstd, rstd_ready)

            def masked(s, n, t, m, bank_at):
                i, turn = bank_at
                for half in range(2):
                    if half == 0:
                        pool.wait_ge(joined_half_ready, head_turn.done(s, n))
                    else:
                        pool.wait_ge(row_taken[i], row_turn[i].done(s, turn))
                    b = slice(half * NB // 2, (half + 1) * NB // 2)
                    nc.gpsimd.tensor_tensor(t[:, b, :], t[:, b, :], m[:, b, :], ALU.add).then_inc(masked_ready, 1)

            def tail(g):
                norm(g, var2_ready, var_eps2, rstd2, rstd2_ready)

            def step(s, slot, a, b, c):
                before, after = (slot + 2) % 3, (slot + 1) % 3
                def sum2():
                    for i in range(2):
                        pool.wait_ge(o_taken[i], o_turn.done(s, C_OUT[1]))
                    nc.gpsimd.tensor_tensor(y2[:], y2[:], x1[before][:], ALU.add).then_inc(sum2_ready, 1)

                if c and tail_of(s):
                    tail(s - 2)
                if b:
                    masked(s, HEAD_1[0], logit[0], mask[slot], ROW_V1[0])
                    masked(s, HEAD_1[1], logit[1], mask[slot], ROW_V1[1])
                    masked(s, HEAD_1[2], logit[0], mask[slot], ROW_V1[2])
                    masked(s, HEAD_1[3], logit[1], mask[slot], ROW_V1[3])
                if c:
                    masked(s, HEAD_2, logit2, mask[before], ROW_V2)
                if a:
                    stage_a(s + 1, after, "sum")
                    stage_a(s + 1, after, "norm")
                    stage_a(s + 1, after, "self edges")
                if c:
                    sum2()

            schedule(pool, stage_a, step, tail)

        @block.scalar
        def _(act):
            act.wait_ge(pool_consts, POOL_CONSTS)

            def stage_a(g, slot, piece):
                if piece == "x":
                    for k in range(KF):
                        act.wait_ge(a_full[k], nth(A_TURNS, g, A_X))
                        nc.scalar.copy(xT[:, k, :], bank_a[k][:]).then_inc(a_taken[k], 1)
                if piece == "mask":
                    act.wait_ge(a_full[0], nth(A_TURNS, g, A_MASK))
                    nc.scalar.copy(mask_T[slot][:, 0:2, :], bank_a[0][:].bitcast(BF16)
                                   .rearrange("p (b n) -> p b n", b=2)).then_inc(a_taken[0], 1)
                if piece == "low":
                    act.wait_ge(a_full[1], nth(A_TURNS, g, A_LOGIT))
                    act.wait_ge(a_taken[0], nth(A_TURNS, g, A_LOGIT))
                    if not (isinstance(g, int) and g == 0):
                        act.wait_ge(prob0_ready, nth(1, g - 1, 0))
                    for b in range(NB):
                        last = nc.scalar.activation(logit0[:, b, :], bank_a[1][:], ACT.Identity,
                                                    bias=sj[:, 1, b:b + 1], scale=SLOPE)
                    last.then_inc(low0_ready, 1)
                if piece == "exp":
                    act.wait_ge(masked0_ready, nth(1, g, 0))
                    for b in range(NB):
                        last = nc.scalar.activation(prob0[:, b, :], logit0[:, b, :], ACT.Exp,
                                                    bias=neg_top0[:, b:b + 1], accum_out=den0[:, b:b + 1])
                    last.then_inc(prob0_ready, 1)
                if piece == "scale":
                    act.wait_ge(rden0_ready, nth(1, g, 0))
                    for b in range(NB):
                        if b % 2 == 0:
                            act.wait_ge(a_full[b // 2], nth(A_TURNS, g, A_VALUES))
                        last = nc.scalar.activation(values0[:, b, :], bank_a[b // 2][:, (b % 2) * F:(b % 2 + 1) * F],
                                                    ACT.Copy, scale=rden0[:, b:b + 1])
                        if b % 2:
                            last.then_inc(a_taken[b // 2], 1)
                for i in range(2):
                    if piece == f"mix {i}":
                        act.wait_ge(a_full[i], nth(A_TURNS, g, A_OUT))
                        nc.scalar.copy(mix0[:, 2 * i:2 * i + 2, :], bank_a[i][:]
                                       .rearrange("p (b f) -> p b f", b=2)).then_inc(a_taken[i], 1)
                if piece == "x1T":
                    act.wait_ge(a_full[0], nth(A_TURNS, g, A_X1T))
                    nc.scalar.copy(x1T[:, 0, :], bank_a[0][:]).then_inc(a_taken[0], 1)

            def low(s, n, t, bias):
                act.wait_ge(v2_full, head_turn.done(s, n))
                act.wait_ge(a_low_ready, layer_turn.done(s, 1 if n == HEAD_2 else 0))
                for half_ready, blocks in ((low_half_ready, (0, 1)), (low_ready, (2, 3))):
                    for b in blocks:
                        last = nc.scalar.activation(t[:, b, :], bank_v2[:], ACT.Identity, bias=bias(b))
                    last.then_inc(half_ready, 1)

            def expo(s, n, dst, src):
                for half in range(2):
                    b = slice(half * NB // 2, (half + 1) * NB // 2)
                    act.wait_ge(masked_ready, half_turn.done(s, 2 * n + half))
                    last = nc.scalar.activation(dst[:, b, :], src[:, b, :], ACT.Exp)
                last.then_inc(prob_ready, 1)

            def take_head(s, n):
                for i in range(2):
                    act.wait_ge(rden_ready, nth(8, s, 2 * n + i))
                    for j in range(2):
                        b = 2 * i + j
                        last = nc.scalar.activation(hid[:, b, n * D:(n + 1) * D],
                                                    bank_o[i][:, j * (D + 1):j * (D + 1) + D],
                                                    ACT.Copy, scale=rden[:, b:b + 1])
                    last.then_inc(o_taken[i], 1)

            def step(s, slot, a, b, c):
                after = (slot + 1) % 3

                def take_xl1(q):
                    act.wait_ge(o_full[q % 2], o_turn.done(s, B_XL[q // 2]))
                    nc.scalar.copy(xl1[:, q, :, 0:D], bank_o[q % 2][:]
                                   .rearrange("p (h f) -> p h f", h=H)).then_inc(o_taken[q % 2], 1)

                def low1(n):
                    if n == 0 and c:
                        act.wait_ge(hid_ready, nth(1, s - 1, 0))
                    if n >= 2:
                        act.wait_ge(prob_ready, head_turn.done(s, HEAD_1[n - 2]))
                    low(s, HEAD_1[n], logit[n % 2], lambda q: a_low[:, q, n:n + 1])

                def expo1(n):
                    if n >= 2:
                        act.wait_ge(o_full[1], o_turn.done(s, B_HEADS[n - 2]))
                    expo(s, HEAD_1[n], prob[n % 2], logit[n % 2])

                def take_hidden_T(half):
                    for k in (2 * half, 2 * half + 1):
                        act.wait_ge(o_full[k % 2], o_turn.done(s, C_HT[half]))
                        nc.scalar.copy(hid_T[:, k, :], bank_o[k % 2][:]).then_inc(o_taken[k % 2], 1)

                def take_xl2(q):
                    act.wait_ge(o_full[q % 2], o_turn.done(s, C_XL[q // 2]))
                    nc.scalar.copy(xl2[:, q, 0:2 + F],
                                   bank_o[q % 2][:, 0:2 + F]).then_inc(o_taken[q % 2], 1)

                def exp_hidden():
                    act.wait_ge(o_taken[1], o_turn.done(s, B_HEADS[3]))
                    nc.scalar.activation(logit[1][:], hid[:], ACT.Exp).then_inc(exp_h_ready, 1)

                def take_product2(half):
                    if half == 0 and not (isinstance(s, int) and s == 1):
                        act.wait_ge(out_ready, nth(1, s - 2, 0))
                    act.wait_ge(rden2_ready, nth(2, s - 1, half))
                    for q in (2 * half, 2 * half + 1):
                        nc.scalar.activation(y2[:, q, :], bank_o[q % 2][:, 0:F], ACT.Copy,
                                             scale=rden2[:, q:q + 1]).then_inc(o_taken[q % 2], 1)

                if c:
                    take_hidden_T(0)
                if a:
                    stage_a(s + 1, after, "x")
                if c:
                    take_hidden_T(1)
                    take_xl2(0)
                    take_xl2(1)
                if a:
                    stage_a(s + 1, after, "mask")
                if b:
                    low1(0)
                if c:
                    take_xl2(2)
                    take_xl2(3)
                if b:
                    low1(1)
                    take_xl1(0)
                    expo1(0)
                if a:
                    stage_a(s + 1, after, "low")
                if b:
                    take_xl1(1)
                    expo1(1)
                    take_xl1(2)
                    take_xl1(3)
                    low1(2)
                if a:
                    stage_a(s + 1, after, "exp")
                if b:
                    take_head(s, 0)
                    low1(3)
                if a:
                    stage_a(s + 1, after, "scale")
                if c:
                    low(s, HEAD_2, logit2, lambda q: a2_low[:, q, :])
                if b:
                    expo1(2)
                    take_head(s, 1)
                if a:
                    stage_a(s + 1, after, "mix 0")
                    stage_a(s + 1, after, "mix 1")
                if b:
                    expo1(3)
                if c:
                    expo(s, HEAD_2, prob2, logit2)
                if b:
                    take_head(s, 2)
                    take_head(s, 3)
                if a:
                    stage_a(s + 1, after, "x1T")
                if b:
                    exp_hidden()
                if c:
                    take_product2(0)
                    take_product2(1)

            schedule(act, stage_a, step, lambda g: None)

        @block.vector
        def _(dve):
            count = [0]

            def const(instruction):
                instruction.then_inc(vector_consts, 1)
                count[0] += 1
                dve.wait_ge(vector_consts, count[0])

            dve.wait_ge(bias3_in, 32)
            const(nc.vector.memset(bias_row[:, HD:HD + 2], 0.0))
            const(nc.vector.tensor_copy(bias_parts[:, 0, :], bias_row))
            const(nc.vector.tensor_tensor(bias_rest, bias_row, bias_parts[:, 0, :], ALU.subtract))
            const(nc.vector.tensor_copy(bias_parts[:, 1, :], bias_rest))
            const(nc.vector.tensor_tensor(bias_rest, bias_rest, bias_parts[:, 1, :], ALU.subtract))
            nc.vector.tensor_copy(bias_parts[:, 2, :], bias_rest).then_inc(bias_parts_ready, 1)
            dve.wait_ge(weights_in, WEIGHTS)

            places = [t[:, b, c:c + F] for t in (logit[0], logit[1], prob[0], prob[1]) for b in range(NB)
                      for c in range(0, N, F)]

            def through(w, vec, dst):
                place = places.pop()
                nc.vector.tensor_tensor_reduce(place[:, 0:w.shape[-1]], w, vec, 1.0, 0.0, ALU.mult,
                                               ALU.add, dst).then_inc(vector_consts, 1)
                count[0] += 1
            for t in range(2):
                for k in range(KF):
                    through(w0_t[:, k, :], vec0[:, t, :], wa0[:, k, t:t + 1])
                    for h in range(H):
                        cols = slice(h * D, (h + 1) * D)
                        through(w1_t[:, k, cols], vec1[:, t, cols], wa1[:, k, t * H + h:t * H + h + 1])
                for k in range(KH):
                    through(w2_t[:, k, 2:], vec2[:, t, :], w2_t[:, k, t:t + 1])
            dve.wait_ge(pool_consts, POOL_CONSTS)
            dve.wait_ge(vector_consts, count[0])
            for k in range(KF):
                const(nc.vector.tensor_scalar(wa0_wide[:, k, :], ones[:], wa0[:, k, 0:1], None, ALU.mult))
            assert count[0] == VECTOR_CONSTS, count[0]

            sa = Steps(dve, a_steps, A_STEPS)
            st_b = Steps(dve, b_steps, B_STEPS)
            st_c = Steps(dve, c_steps, C_STEPS)
            st_n = Steps(dve, n_steps, N_STEPS)

            def gate(slot):
                nc.vector.memset(gate_t[:, slot:slot + 1], 0.0)

            def moments_of(st, slot, src, stats_t, moments_t, var_t, var_sem):
                for b in range(NB):
                    st.done(nc.vector.bn_stats(stats_t[:, b, :], src[:, b, :]))
                st.wait()
                gate(slot)
                for b in range(NB):
                    st.done(nc.vector.bn_aggr(moments_t[:, b, :], stats_t[:, b, :]))
                st.wait()
                nc.vector.tensor_scalar(var_t[:], moments_t[:, :, 1], EPS, None, ALU.add).then_inc(var_sem, 1)

            def normed(g, src, moments_t, rstd_t, rstd_sem, dst, ready):
                dve.wait_ge(rstd_sem, nth(1, g, 0))
                for b in range(NB):
                    last = nc.vector.tensor_scalar(dst[:, b, :], src[:, b, :], moments_t[:, b, 0:1],
                                                   rstd_t[:, b:b + 1], ALU.subtract, ALU.mult)
                last.then_inc(ready, 1)

            def stage_a(g, slot, piece):
                if piece == "make mask":
                    sa.begin(g)
                    dve.wait_ge(adj_in, nth(16, g, 15))
                    if not (isinstance(g, int) and g < 3):
                        dve.wait_ge(masked_ready, half_turn.done(g - 2, 2 * HEAD_2 + 1))
                    nc.vector.tensor_scalar(mask[slot][:], adj_t[:], 0.0, NO_EDGE, ALU.is_le,
                                            ALU.mult).then_inc(mask_ready, 1)
                if piece == "mask":
                    dve.wait_ge(a_full[1], nth(A_TURNS, g, A_MASK))
                    nc.vector.tensor_copy(mask_T[slot][:, 2:4, :], bank_a[1][:].bitcast(BF16)
                                          .rearrange("p (b n) -> p b n", b=2)).then_inc(a_taken[1], 1)
                if piece == "s_j":
                    dve.wait_ge(a_full[0], nth(A_TURNS, g, A_LOGIT))
                    sa.done(nc.vector.tensor_copy(sj[:, 0, :], bank_a[0][:, 0:NB]))
                    nc.vector.tensor_scalar(sj[:, 1, :], bank_a[0][:, 0:NB], SLOPE, None,
                                            ALU.mult).then_inc(a_taken[0], 1)
                if piece == "joined":
                    sa.wait()
                    dve.wait_ge(low0_ready, nth(1, g, 0))
                    for b in range(NB):
                        last = nc.vector.scalar_tensor_tensor(out=logit0[:, b, :], in0=bank_a[1][:],
                                                              scalar=sj[:, 0, b:b + 1], in1=logit0[:, b, :],
                                                              op0=ALU.add, op1=ALU.max)
                    last.then_inc(a_taken[1], 1)
                    dve.wait_ge(a_taken[0], nth(A_TURNS, g, A_MASK))
                    dve.wait_ge(a_taken[1], nth(A_TURNS, g, A_LOGIT))
                    gate(5)
                    for b in range(NB):
                        sa.done(nc.vector.tensor_tensor_reduce(logit0[:, b, :], logit0[:, b, :],
                                                               mask_T[slot][:, b, :], 1.0, LOWEST, ALU.add,
                                                               ALU.max, top0[:, b:b + 1]))
                    sa.wait()
                    nc.vector.tensor_scalar(neg_top0[:], top0[:], -1.0, None,
                                            ALU.mult).then_inc(masked0_ready, 1)
                if piece == "1 / den":
                    dve.wait_ge(prob0_ready, nth(1, g, 0))
                    nc.vector.reciprocal(rden0[:], den0[:]).then_inc(rden0_ready, 1)

                if piece == "leaky":
                    for i in range(2):
                        dve.wait_ge(a_taken[i], nth(A_TURNS, g, A_OUT))
                    nc.vector.scalar_tensor_tensor(out=leak0[:], in0=mix0[:], scalar=SLOPE, in1=mix0[:],
                                                   op0=ALU.mult, op1=ALU.max).then_inc(leak0_ready, 1)
                if piece == "x1T":
                    dve.wait_ge(a_full[1], nth(A_TURNS, g, A_X1T))
                    nc.vector.tensor_copy(x1T[:, 1, :], bank_a[1][:]).then_inc(a_taken[1], 1)
                if piece == "cols":
                    st_b.begin(g)
                    cols1(g)
                if piece == "rows":
                    small_rows(g, AROW1, a_rows, 3 * H)

            def moments_a(g):
                dve.wait_ge(sum0_ready, nth(1, g, 0))
                moments_of(sa, 6, leak0, stats, moments, var_eps, var_ready)

            def normed_a(g, slot):
                normed(g, leak0, moments, rstd, rstd_ready, x1[slot], x1_ready)
                sa.end()

            def split(st, src, r, parts, n):
                st.done(nc.vector.tensor_copy(parts[:, :, 0:n], src))
                st.wait()
                st.done(nc.vector.tensor_tensor(r, src, parts[:, :, 0:n], ALU.subtract))
                st.wait()
                st.done(nc.vector.tensor_copy(parts[:, :, n:2 * n], r))
                st.wait()
                st.done(nc.vector.tensor_tensor(r, r, parts[:, :, n:2 * n], ALU.subtract))
                st.wait()
                nc.vector.tensor_copy(parts[:, :, 2 * n:3 * n], r).then_inc(parts_ready, 1)

            def maxima(s, m, slot_g, top_of, bank_at):
                i, turn = bank_at
                dve.wait_ge(row_full[i], row_turn[i].done(s, turn))
                gate(slot_g)
                for b in range(NB):
                    last = nc.vector.tensor_tensor_reduce(junk[:, i, b, :], bank_row[i][:], m[:, b, :], 1.0,
                                                          LOWEST, ALU.add, ALU.max, top_of(b))
                last.then_inc(row_taken[i], 1)

            def shifts(st, b_cols, n, t, c, vv, r, parts):
                st.done(nc.vector.tensor_tensor(t, t, b_cols, ALU.add))
                st.wait()
                st.done(nc.vector.scalar_tensor_tensor(out=c, in0=t, scalar=SLOPE, in1=t, op0=ALU.mult,
                                                       op1=ALU.max))
                st.wait()
                st.done(nc.vector.tensor_tensor(vv[:, :, 0:n], b_cols, c, ALU.subtract))
                st.done(nc.vector.scalar_tensor_tensor(out=vv[:, :, n:2 * n], in0=b_cols, scalar=SLOPE,
                                                       in1=c, op0=ALU.mult, op1=ALU.subtract))
                st.wait()
                split(st, vv[:], r, parts, 2 * n)

            def joined(s, n, t, bank_at, a_of):
                i, turn = bank_at
                dve.wait_ge(row_full[i], row_turn[i].done(s, turn))
                for low_half, half_ready, blocks in ((low_half_ready, joined_half_ready, (0, 1)),
                                                     (low_ready, row_taken[i], (2, 3))):
                    dve.wait_ge(low_half, head_turn.done(s, n))
                    for b in blocks:
                        last = nc.vector.scalar_tensor_tensor(out=t[:, b, :], in0=bank_row[i][:], scalar=a_of(b),
                                                              in1=t[:, b, :], op0=ALU.add, op1=ALU.max)
                    last.then_inc(half_ready, 1)

            def denominators(s, n):
                for i in range(2):
                    dve.wait_ge(o_full[i], o_turn.done(s, B_HEADS[n]))
                    if n:
                        dve.wait_ge(o_taken[i], o_turn.done(s, B_HEADS[n - 1]))
                    den = bank_o[i][:, 0:2 * (D + 1)].rearrange("p (b f) -> p b f", b=2)[:, :, D]
                    nc.vector.reciprocal(rden[:, 2 * i:2 * i + 2], den).then_inc(rden_ready, 1)

            def small_rows(s, turn, dst, n):
                dve.wait_ge(small_full, small_turn.done(s, turn))
                nc.vector.tensor_copy(dst[:], bank_small[0:n, 0:N // 2].bitcast(BF16)).then_inc(small_taken, 1)

            def cols1(s):
                dve.wait_ge(small_full, small_turn.done(s, COLS1))
                nc.vector.tensor_copy(ab[:], bank_small[:, 0:NB * 2 * H]
                                      .rearrange("p (b c) -> p b c", b=NB)).then_inc(small_taken, 1)
                dve.wait_ge(small_taken, small_turn.done(s, COLS1))
                nc.vector.tensor_scalar(a_low[:], ab[:, :, 0:H], SLOPE, None, ALU.mult).then_inc(a_low_ready, 1)
                split(st_b, ab[:, :, 0:H], rest[:, :, 0:H], a_parts, H)

            def cols2(s):
                st_c.begin(s - 1)
                for i in range(2):
                    dve.wait_ge(o_taken[i], o_turn.done(s, C_XL[1]))
                nc.vector.tensor_scalar(a2_low[:], xl2[:, :, 0:1], SLOPE, None, ALU.mult).then_inc(a_low_ready, 1)
                split(st_c, xl2[:, :, 0:1], rest2[:, :, 0:1], a2_parts, 1)

            def denominators2(g, half):
                for i in range(2):
                    q = 2 * half + i
                    dve.wait_ge(o_full[i], o_turn.done(g + 1, C_OUT[half]))
                    last = nc.vector.reciprocal(rden2[:, q:q + 1], bank_o[i][:, F:F + 1])
                last.then_inc(rden2_ready, 1)

            def tail_moments(g):
                st_n.begin(g)
                dve.wait_ge(sum2_ready, nth(1, g, 0))
                moments_of(st_n, 7, y2, stats2, moments2, var_eps2, var2_ready)
                st_n.end()

            def tail_normed(g):
                if not (isinstance(g, int) and g == 0):
                    dve.wait_ge(out_stored, nth(16, g - 1, 15))
                normed(g, y2, moments2, rstd2, rstd2_ready, out_t, out_ready)

            def step(s, slot, a, b, c):
                before, after = (slot + 2) % 3, (slot + 1) % 3

                def maxima1(n):
                    if n == 0:
                        dve.wait_ge(self_edges, nth(1, s, 0))
                    maxima(s, mask_T[slot], n, lambda q: top[:, q, n:n + 1], ROW_A1[n])

                def joined1(n):
                    joined(s, HEAD_1[n], logit[n % 2], ROW_V1[n], lambda q: ab[:, q, n:n + 1])

                def elu_low():
                    dve.wait_ge(exp_h_ready, nth(1, s - 1, 0))
                    dve.wait_ge(elu_high_ready, nth(1, s - 1, 0))
                    nc.vector.scalar_tensor_tensor(out=hid[:], in0=logit[1][:], scalar=1.0, in1=logit[0][:],
                                                   op0=ALU.min, op1=ALU.add).then_inc(hid_ready, 1)

                def elu_high():
                    for i in range(2):
                        dve.wait_ge(o_taken[i], o_turn.done(s, B_HEADS[3]))
                    nc.vector.tensor_scalar(logit[0][:], hid[:], 0.0, -1.0, ALU.max,
                                            ALU.add).then_inc(elu_high_ready, 1)

                def shifts1():
                    for i in range(2):
                        dve.wait_ge(row_taken[i], row_turn[i].done(s, 1))
                    st_b.resume(s)
                    shifts(st_b, ab[:, :, H:2 * H], H, top[:], shift[:], v, rest[:], v_parts)
                    st_b.end()

                def maxima2():
                    maxima(s, mask_T[before], 4, lambda q: top2[:, q, :], ROW_A2)

                def shifts2():
                    dve.wait_ge(row_taken[0], row_turn[0].done(s, ROW_A2[1]))
                    shifts(st_c, xl2[:, :, 1:2], 1, top2[:], shift2[:], v_2, rest2[:], v2_parts)
                    st_c.end()

                def joined2():
                    joined(s, HEAD_2, logit2, ROW_V2, lambda q: xl2[:, q, 0:1])

                if c:
                    elu_low()
                if c and tail_of(s):
                    denominators2(s - 2, 0)
                if b:
                    maxima1(0)
                    maxima1(1)
                if c and tail_of(s):
                    denominators2(s - 2, 1)
                if a:
                    stage_a(s + 1, after, "make mask")
                if b:
                    maxima1(2)
                    maxima1(3)
                    shifts1()
                if a:
                    stage_a(s + 1, after, "mask")
                if b:
                    small_rows(s, VROW1, v_rows, 6 * H)
                if c and tail_of(s):
                    tail_moments(s - 2)
                if b:
                    joined1(0)
                if c:
                    cols2(s)
                if a:
                    stage_a(s + 1, after, "s_j")
                if b:
                    joined1(1)
                if c:
                    small_rows(s, AROW2, a2_rows, 3)
                if a:
                    stage_a(s + 1, after, "joined")
                if c:
                    maxima2()
                if b:
                    denominators(s, 0)
                if c:
                    shifts2()
                if b:
                    joined1(2)
                if a:
                    stage_a(s + 1, after, "1 / den")
                if c:
                    small_rows(s, VROW2, v2_rows, 6)
                if b:
                    joined1(3)
                if c:
                    joined2()
                if c and tail_of(s):
                    tail_normed(s - 2)
                if b:
                    denominators(s, 1)
                if a:
                    stage_a(s + 1, after, "leaky")
                if b:
                    denominators(s, 2)
                if a:
                    moments_a(s + 1)
                    normed_a(s + 1, after)
                if b:
                    denominators(s, 3)
                if a:
                    stage_a(s + 1, after, "x1T")
                if b:
                    elu_high()
                if a:
                    stage_a(s + 1, after, "cols")
                    stage_a(s + 1, after, "rows")

            def finish(g):
                denominators2(g, 0)
                denominators2(g, 1)
                tail_moments(g)
                tail_normed(g)

            def stage_a_whole(g, slot, piece):
                stage_a(g, slot, piece)
                if piece == "norm":
                    moments_a(g)
                    normed_a(g, slot)

            schedule(dve, stage_a_whole, step, finish)

        @block.tensor
        def _(pe):
            pe.wait_ge(pool_consts, POOL_CONSTS)

            def a_free(i, g, turn):
                if turn or not (isinstance(g, int) and g == 0):
                    pe.wait_ge(a_taken[i], g * A_TURNS + turn)

            def free(semaphore, turns, s, turn):
                n = turns.before(s, turn)
                if not (isinstance(n, int) and n == 0):
                    pe.wait_ge(semaphore, n)

            def stage_a(g, slot, piece):
                if piece == "x":
                    pe.wait_ge(x_in, nth(16, g, 15))
                    for k in range(KF):
                        a_free(k, g, A_X)
                        for b in range(NB):
                            last = nc.tensor.transpose(bank_a[k][:, b * P:(b + 1) * P],
                                                       x_t[:, b, k * P:(k + 1) * P], ident[:])
                        last.then_inc(a_full[k], 1)
                if piece == "mask":
                    pe.wait_ge(mask_ready, nth(1, g, 0))
                    for i in range(2):
                        a_free(i, g, A_MASK)
                        rows = bank_a[i][:].bitcast(BF16).rearrange("p (b n) -> p b n", b=2)
                        for j in range(2):
                            for b in range(NB):
                                d = 2 * i + j
                                last = nc.tensor.transpose(rows[:, j, b * P:(b + 1) * P],
                                                           mask[slot][:, b, d * P:(d + 1) * P], ident_b[:])
                        last.then_inc(a_full[i], 1)
                if piece == "s_j":
                    if isinstance(g, int) and g == 0:
                        pe.wait_ge(vector_consts, VECTOR_CONSTS)
                        pe.wait_ge(weights_in, WEIGHTS)
                        pe.wait_ge(bias3_in, 3 * 16)
                    pe.wait_ge(a_taken[1], nth(A_TURNS, g, A_X))
                    a_free(0, g, A_LOGIT)
                    for b in range(NB):
                        for k in range(KF):
                            last = nc.tensor.matmul(bank_a[0][:, b:b + 1], xT[:, k, b * P:(b + 1) * P],
                                                    wa0[:, k, 1:2], start=(k == 0), stop=(k == KF - 1))
                    last.then_inc(a_full[0], 1)
                if piece == "s_i":
                    pe.wait_ge(a_taken[0], nth(A_TURNS, g, A_X))
                    a_free(1, g, A_LOGIT)
                    for k in range(KF):
                        last = nc.tensor.matmul(bank_a[1][:], wa0_wide[:, k, :], xT[:, k, :],
                                                start=(k == 0), stop=(k == KF - 1))
                    last.then_inc(a_full[1], 1)
                if piece == "values":
                    for i in range(2):
                        a_free(i, g, A_VALUES)
                    for b in range(NB):
                        for k in range(KF):
                            last = nc.tensor.matmul(bank_a[b // 2][:, (b % 2) * F:(b % 2 + 1) * F],
                                                    xT[:, k, b * P:(b + 1) * P], w0_t[:, k, :],
                                                    start=(k == 0), stop=(k == KF - 1))
                        if b % 2:
                            last.then_inc(a_full[b // 2], 1)
                if piece == "attention":
                    pe.wait_ge(prob0_ready, nth(1, g, 0))
                    for i in range(2):
                        a_free(i, g, A_OUT)
                    for b in range(NB):
                        for k in range(NB):
                            last = nc.tensor.matmul(bank_a[b // 2][:, (b % 2) * F:(b % 2 + 1) * F],
                                                    prob0[:, k, b * P:(b + 1) * P], values0[:, k, :],
                                                    start=(k == 0), stop=(k == NB - 1))
                        if b % 2:
                            last.then_inc(a_full[b // 2], 1)
                if piece == "x1T":
                    pe.wait_ge(x1_ready, nth(1, g, 0))
                    for k in range(KF):
                        a_free(k, g, A_X1T)
                        for b in range(NB):
                            last = nc.tensor.transpose(bank_a[k][:, b * P:(b + 1) * P],
                                                       x1[slot][:, b, k * P:(k + 1) * P], ident[:])
                        last.then_inc(a_full[k], 1)
                if piece == "cols":
                    for k in range(KF):
                        pe.wait_ge(a_taken[k], nth(A_TURNS, g, A_X1T))
                    free(small_taken, small_turn, g, COLS1)
                    for q in range(NB):
                        for k in range(KF):
                            last = nc.tensor.matmul(bank_small[:, q * 2 * H:(q + 1) * 2 * H],
                                                    x1T[:, k, q * P:(q + 1) * P], wa1[:, k, :],
                                                    start=(k == 0), stop=(k == KF - 1))
                    last.then_inc(small_full, 1)
                if piece == "rows":
                    small(g, AROW1, PARTS_A1, a_parts, 3 * H)
                if piece == "row 0":
                    pe.wait_ge(small_taken, small_turn.done(g, AROW1))
                    row(g, ROW_A1[0], pick_a1, 0, a_rows)
                if piece == "row 1":
                    pe.wait_ge(small_taken, small_turn.done(g, AROW1))
                    row(g, ROW_A1[1], pick_a1, 1, a_rows)
                if piece == "row 2":
                    row(g, ROW_A1[2], pick_a1, 2, a_rows)
                if piece == "row 3":
                    row(g, ROW_A1[3], pick_a1, 3, a_rows)

            def small(s, turn, ready, parts, n):
                pe.wait_ge(parts_ready, parts_turn.done(s, ready))
                free(small_taken, small_turn, s, turn)
                rows = bank_small[0:n, 0:N // 2].bitcast(BF16)
                for b in range(NB):
                    last = nc.tensor.transpose(rows[:, b * P:(b + 1) * P], parts[:, b, :], ident_b[:])
                last.then_inc(small_full, 1)

            def row(s, bank_at, pick, q, rows):
                i, turn = bank_at
                free(row_taken[i], row_turn[i], s, turn)
                nc.tensor.matmul(bank_row[i][:], pick[:, q, :], rows[:], start=True,
                                 stop=True).then_inc(row_full[i], 1)

            def logit_rows(s, n, bank_at, pick, q, rows):
                row(s, bank_at, pick, q, rows)
                free(low_ready, head_turn, s, n)
                nc.tensor.matmul(bank_v2[:], pick[:, q + pick.shape[1] // 2, :], rows[:], start=True,
                                 stop=True).then_inc(v2_full, 1)

            def step(s, slot, a, b, c):
                after = (slot + 1) % 3

                def xl2_block(q):
                    i = q % 2
                    if q == 0:
                        pe.wait_ge(o_taken[1], o_turn.done(s, C_HT[1]))
                    free(o_taken[i], o_turn, s, C_XL[q // 2])
                    nc.tensor.matmul(bank_o[i][:, 0:2 + F], ones3[:], bias3[:, HD:], start=True, stop=False)
                    for k in range(KH):
                        last = nc.tensor.matmul(bank_o[i][:, 0:2 + F], hid_T[:, k, q * P:(q + 1) * P],
                                                w2_t[:, k, :], start=False, stop=(k == KH - 1))
                    last.then_inc(o_full[i], 1)

                def xl1_block(q):
                    free(o_taken[q % 2], o_turn, s, B_XL[q // 2])
                    nc.tensor.matmul(bank_o[q % 2][:], ones3[:], bias3[:, 0:HD], start=True, stop=False)
                    for k in range(KF):
                        last = nc.tensor.matmul(bank_o[q % 2][:], x1T[:, k, q * P:(q + 1) * P], w1_t[:, k, :],
                                                start=False, stop=(k == KF - 1))
                    last.then_inc(o_full[q % 2], 1)

                def product2(q):
                    i = q % 2
                    if q == 0:
                        pe.wait_ge(prob_ready, head_turn.done(s, HEAD_2))
                    free(o_taken[i], o_turn, s, C_OUT[q // 2])
                    for k in range(NB):
                        last = nc.tensor.matmul(bank_o[i][:, 0:F + 1], prob2[:, k, q * P:(q + 1) * P],
                                                xl2[:, k, 2:], start=(k == 0), stop=(k == NB - 1))
                    last.then_inc(o_full[i], 1)

                def rows1(n):
                    if n == 0:
                        pe.wait_ge(small_taken, small_turn.done(s, VROW1))
                    logit_rows(s, HEAD_1[n], ROW_V1[n], pick_v1, n, v_rows)

                def head(n):
                    if n == 0:
                        pe.wait_ge(o_taken[1], o_turn.done(s, B_XL[1]))
                    pe.wait_ge(prob_ready, head_turn.done(s, HEAD_1[n]))
                    for q in range(NB):
                        i = q // 2
                        if q % 2 == 0:
                            free(o_taken[i], o_turn, s, B_HEADS[n])
                        for k in range(NB):
                            last = nc.tensor.matmul(bank_o[i][:, (q % 2) * (D + 1):(q % 2 + 1) * (D + 1)],
                                                    prob[n % 2][:, k, q * P:(q + 1) * P], xl1[:, k, n, :],
                                                    start=(k == 0), stop=(k == NB - 1))
                        if q % 2:
                            last.then_inc(o_full[i], 1)

                def hidden_T(half):
                    pe.wait_ge(hid_ready, nth(1, s - 1, 0))
                    for k in (2 * half, 2 * half + 1):
                        free(o_taken[k % 2], o_turn, s, C_HT[half])
                        for q in range(NB):
                            last = nc.tensor.transpose(bank_o[k % 2][:, q * P:(q + 1) * P],
                                                       hid[:, q, k * P:(k + 1) * P], ident[:])
                        last.then_inc(o_full[k % 2], 1)

                def rows2_a():
                    pe.wait_ge(small_taken, small_turn.done(s, AROW2))
                    row(s, ROW_A2, pick_a2, 0, a2_rows)

                def rows2_v():
                    pe.wait_ge(small_taken, small_turn.done(s, VROW2))
                    logit_rows(s, HEAD_2, ROW_V2, pick_v2, 0, v2_rows)

                if c:
                    hidden_T(0)
                if a:
                    stage_a(s + 1, after, "x")
                if c:
                    hidden_T(1)
                if a:
                    stage_a(s + 1, after, "mask")
                if c:
                    xl2_block(0)
                    xl2_block(1)
                if b:
                    small(s, VROW1, PARTS_V1, v_parts, 6 * H)
                if c:
                    xl2_block(2)
                if b:
                    rows1(0)
                if c:
                    xl2_block(3)
                if a:
                    stage_a(s + 1, after, "s_j")
                if b:
                    rows1(1)
                    xl1_block(0)
                if c:
                    small(s, AROW2, PARTS_A2, a2_parts, 3)
                if a:
                    stage_a(s + 1, after, "s_i")
                if b:
                    xl1_block(1)
                    xl1_block(2)
                    xl1_block(3)
                    rows1(2)
                if c:
                    rows2_a()
                if b:
                    head(0)
                if a:
                    stage_a(s + 1, after, "values")
                if b:
                    rows1(3)
                if c:
                    small(s, VROW2, PARTS_V2, v2_parts, 6)
                if b:
                    head(1)
                if c:
                    rows2_v()
                if a:
                    stage_a(s + 1, after, "attention")
                if b:
                    head(2)
                    head(3)
                if a:
                    stage_a(s + 1, after, "x1T")
                    stage_a(s + 1, after, "cols")
                if c:
                    product2(0)
                if a:
                    stage_a(s + 1, after, "rows")
                if c:
                    product2(1)
                if a:
                    stage_a(s + 1, after, "row 1")
                    stage_a(s + 1, after, "row 0")
                if c:
                    product2(2)
                if a:
                    stage_a(s + 1, after, "row 2")
                if c:
                    product2(3)
                if a:
                    stage_a(s + 1, after, "row 3")

            schedule(pe, stage_a, step, lambda g: None)


_INS = ['x', 'adj', 'L0_gnn_W', 'L0_gnn_a', 'L1_gnn_W1', 'L1_gnn_att_src1', 'L1_gnn_att_dst1', 'L1_gnn_b1',
        'L1_gnn_W2', 'L1_gnn_att_src2', 'L1_gnn_att_dst2', 'L1_gnn_b2']


def kernel(**inputs):
    import numpy as _np
    import concourse.bacc as _bacc
    from concourse.bass_utils import run_bass_kernel_spmd as _run

    nc = _bacc.Bacc("TRN2", target_bir_lowering=False, num_devices=1)
    arrays, args = {}, []
    for name in _INS:
        a = _np.ascontiguousarray(inputs[name])
        arrays[f"in_{name}_dram"] = a
        args.append(nc.dram_tensor(f"in_{name}_dram", a.shape, mybir.dt.from_np(a.dtype), kind="ExternalInput").ap())
    args.append(nc.dram_tensor("out_0_dram", inputs['x'].shape, F32, kind="ExternalOutput").ap())
    build(nc, *args)
    r = _run(nc, [arrays], core_ids=[0])
    return r.results[0]["out_0_dram"]
```
